# Optimizing a Trainium2 kernel written in Bass

```python
import numpy as np
import jax
import jax.numpy as jnp

def _softmax(x, axis=-1):
    return jax.nn.softmax(x, axis=axis)

def _gelu(x):
    return jax.nn.gelu(x, approximate=True)

def _silu(x):
    return jax.nn.silu(x)

def _sigmoid(x):
    return jax.nn.sigmoid(x)

def _layernorm(x, axis=-1, eps=1e-05):
    m = jnp.mean(x, axis=axis, keepdims=True)
    v = jnp.var(x, axis=axis, keepdims=True)
    return (x - m) / jnp.sqrt(v + eps)

def _scatter_add(tgt, idx, src, axis=0):
    return tgt.at[idx].add(src)

def _segment_sum(src, seg, n):
    return jax.ops.segment_sum(src, seg, n)
kernel_name = 'mk_prb_d1_jaxref_r8_09409d'

def setup_inputs(seed: int=0):
    np.random.seed(seed)
    _w = jnp.asarray

    def _L0_attn_setup():
        import jax, jax.numpy as jnp
        import numpy as np
        import math
        HIDDEN = 128
        HEADS = 16
        HEAD_DIM = HIDDEN // HEADS
        B, S = (2, 256)

        def _xavier(key, shape):
            fan_in, fan_out = (shape[1], shape[0])
            limit = math.sqrt(6.0 / (fan_in + fan_out))
            return jax.random.uniform(key, shape, jnp.float32, -limit, limit)
        key = jax.random.key(seed)
        ks = jax.random.split(key, 5)
        x = jax.random.normal(ks[0], (B, S, HIDDEN), jnp.float32)
        Wq = _xavier(ks[1], (HIDDEN, HIDDEN))
        Wk = _xavier(ks[2], (HIDDEN, HIDDEN))
        Wv = _xavier(ks[3], (HIDDEN, HIDDEN))
        Wo = _xavier(ks[4], (HIDDEN, HIDDEN))
        bq = jnp.zeros((HIDDEN,), jnp.float32)
        bk = jnp.zeros((HIDDEN,), jnp.float32)
        bv = jnp.zeros((HIDDEN,), jnp.float32)
        bo = jnp.zeros((HIDDEN,), jnp.float32)
        return {'x': x, 'Wq': Wq, 'bq': bq, 'Wk': Wk, 'bk': bk, 'Wv': Wv, 'bv': bv, 'Wo': Wo, 'bo': bo}
    _L0_attn_in = _L0_attn_setup()

    def _L0_ffn_setup():
        import jax, jax.numpy as jnp
        import numpy as np
        D_MODEL = 128
        HIDDEN = 256
        N_EXPERTS = 8
        TOP_K = 2
        BATCH = 2
        SEQ = 256
        key = jax.random.key(seed)
        ks = jax.random.split(key, 9)
        s = 0.02
        return {'x': jax.random.normal(ks[0], (BATCH, SEQ, D_MODEL), dtype=jnp.float32), 'w_router': jax.random.normal(ks[1], (D_MODEL, N_EXPERTS), dtype=jnp.float32) * s, 'w1': jax.random.normal(ks[2], (N_EXPERTS, D_MODEL, HIDDEN), dtype=jnp.float32) * s, 'w3': jax.random.normal(ks[3], (N_EXPERTS, D_MODEL, HIDDEN), dtype=jnp.float32) * s, 'w2': jax.random.normal(ks[4], (N_EXPERTS, HIDDEN, D_MODEL), dtype=jnp.float32) * s, 'sw1': jax.random.normal(ks[5], (D_MODEL, HIDDEN), dtype=jnp.float32) * s, 'sw3': jax.random.normal(ks[6], (D_MODEL, HIDDEN), dtype=jnp.float32) * s, 'sw2': jax.random.normal(ks[7], (HIDDEN, D_MODEL), dtype=jnp.float32) * s}
    _L0_ffn_in = _L0_ffn_setup()
    _d = {'L0_attn_x': _L0_attn_in['x'], 'L0_attn_Wq': _L0_attn_in['Wq'], 'L0_attn_bq': _L0_attn_in['bq'], 'L0_attn_Wk': _L0_attn_in['Wk'], 'L0_attn_bk': _L0_attn_in['bk'], 'L0_attn_Wv': _L0_attn_in['Wv'], 'L0_attn_bv': _L0_attn_in['bv'], 'L0_attn_Wo': _L0_attn_in['Wo'], 'L0_attn_bo': _L0_attn_in['bo'], 'L0_ffn_w_router': _L0_ffn_in['w_router'], 'L0_ffn_w1': _L0_ffn_in['w1'], 'L0_ffn_w3': _L0_ffn_in['w3'], 'L0_ffn_w2': _L0_ffn_in['w2'], 'L0_ffn_sw1': _L0_ffn_in['sw1'], 'L0_ffn_sw3': _L0_ffn_in['sw3'], 'L0_ffn_sw2': _L0_ffn_in['sw2']}
    _x0 = _d['L0_attn_x']
    _d['L0_attn_x'] = jax.random.normal(jax.random.fold_in(jax.random.key(seed), 1), (32, 256, 128), dtype=_x0.dtype)
    del _x0
    return _d

def reference(L0_attn_x, L0_attn_Wq, L0_attn_bq, L0_attn_Wk, L0_attn_bk, L0_attn_Wv, L0_attn_bv, L0_attn_Wo, L0_attn_bo, L0_ffn_w_router, L0_ffn_w1, L0_ffn_w3, L0_ffn_w2, L0_ffn_sw1, L0_ffn_sw3, L0_ffn_sw2):

    def _L0_attn_ref(x, Wq, bq, Wk, bk, Wv, bv, Wo, bo):
        import jax, jax.numpy as jnp
        import numpy as np
        import math
        HIDDEN = 128
        HEADS = 16
        HEAD_DIM = HIDDEN // HEADS
        B, S = (2, 256)

        def _xavier(key, shape):
            fan_in, fan_out = (shape[1], shape[0])
            limit = math.sqrt(6.0 / (fan_in + fan_out))
            return jax.random.uniform(key, shape, jnp.float32, -limit, limit)
        b, s, d = x.shape
        h, hd = (HEADS, HEAD_DIM)
        q = (x @ Wq.T + bq).reshape(b, s, h, hd).transpose(0, 2, 1, 3)
        k = (x @ Wk.T + bk).reshape(b, s, h, hd).transpose(0, 2, 1, 3)
        v = (x @ Wv.T + bv).reshape(b, s, h, hd).transpose(0, 2, 1, 3)
        scores = jnp.einsum('bhqd,bhkd->bhqk', q, k) / math.sqrt(hd)
        causal = jnp.tril(jnp.ones((s, s), bool))
        scores = jnp.where(causal, scores, -jnp.inf)
        attn = jax.nn.softmax(scores, axis=-1)
        out = jnp.einsum('bhqk,bhkd->bhqd', attn, v)
        out = out.transpose(0, 2, 1, 3).reshape(b, s, d)
        return out @ Wo.T + bo

    def _L0_ffn_ref(x, w_router, w1, w3, w2, sw1, sw3, sw2):
        import jax, jax.numpy as jnp
        import numpy as np
        D_MODEL = 128
        HIDDEN = 256
        N_EXPERTS = 8
        TOP_K = 2
        BATCH = 2
        SEQ = 256
        b, s, d = x.shape
        xf = x.reshape(b * s, d)
        probs = jax.nn.softmax(xf @ w_router, axis=-1)
        top_vals, top_idx = jax.lax.top_k(probs, TOP_K)
        gates = top_vals / jnp.sum(top_vals, axis=-1, keepdims=True)
        onehot = jax.nn.one_hot(top_idx, N_EXPERTS, dtype=xf.dtype)
        cw = jnp.einsum('tk,tke->te', gates, onehot)
        h1 = jnp.einsum('td,edh->eth', xf, w1)
        h3 = jnp.einsum('td,edh->eth', xf, w3)
        y = jnp.einsum('eth,ehd->etd', jax.nn.silu(h1) * h3, w2)
        out = jnp.einsum('etd,te->td', y, cw)
        out = out + jax.nn.silu(xf @ sw1) * (xf @ sw3) @ sw2
        return out.reshape(b, s, d)
    x = L0_attn_x
    xn = _layernorm(x, axis=-1)
    x = x + _L0_attn_ref(xn, L0_attn_Wq, L0_attn_bq, L0_attn_Wk, L0_attn_bk, L0_attn_Wv, L0_attn_bv, L0_attn_Wo, L0_attn_bo) + _L0_ffn_ref(xn, L0_ffn_w_router, L0_ffn_w1, L0_ffn_w3, L0_ffn_w2, L0_ffn_sw1, L0_ffn_sw3, L0_ffn_sw2)
    return x

_drawn_inputs = setup_inputs


def setup_inputs(seed=0):
    import zlib

    import numpy as np

    out = dict(_drawn_inputs(seed))
    spreads = {'L0_attn_bq': (0.0, 2.0),
     'L0_attn_bk': (0.0, 2.0),
     'L0_attn_bv': (0.0, 0.498),
     'L0_attn_bo': (0.0, 0.47)}
    factors = {'L0_ffn_w_router': 8.0,
     'L0_ffn_w1': 8.0,
     'L0_ffn_w3': 8.0,
     'L0_ffn_w2': 8.0,
     'L0_ffn_sw1': 7.163,
     'L0_ffn_sw3': 7.062,
     'L0_ffn_sw2': 7.083}
    for name, (base, spread) in spreads.items():
        noise = np.random.default_rng([zlib.crc32(name.encode()), seed]).standard_normal(out[name].shape)
        drawn = base * np.exp(spread * noise) if base else spread * noise
        out[name] = jnp.asarray(drawn.astype(out[name].dtype))
    for name, factor in factors.items():
        out[name] = (out[name] * factor).astype(out[name].dtype)
    return out
```

```python
from contextlib import ExitStack

import concourse.bass as bass
from concourse import mybir

F32 = mybir.dt.float32
F32R = mybir.dt.float32r
BF16 = mybir.dt.bfloat16
U32 = mybir.dt.uint32
ALU = mybir.AluOpType
ACT = mybir.ActivationFunctionType
AX = mybir.AxisListType

P = 128
BANK = 512
NJ = 4
ROWS = P // NJ
EPS = 1e-5
MASKED = -3.0e38


def program(nc, x, wq, bq, wk, bk, wv, bv, wo, bo, w_router, w1, w3, w2, sw1, sw3, sw2, out):
    B, S, D = x.shape
    E, _, HID = w1.shape
    HD = 8
    H = D // HD
    NG = H // NJ
    SEQS = 2
    T = SEQS * S
    NT = T // P
    QT = S // P
    GROUPS = B // SEQS
    NE = E + 1
    NH = HID // P
    STEPS = NE * NH
    PAIRS = NG * SEQS * NJ // 2
    UNITS = SEQS * 3
    SLOTS = 4
    SCALE = float(HD) ** -0.5
    ONE = 3 * HD
    assert D == P and T == BANK and QT == 2 and NH == 2 and GROUPS % 2 == 0 and E == 8

    x_v = x.rearrange("(g s) (t p) d -> g p (s t) d", s=SEQS, p=P)
    out_v = out.rearrange("(g s) (t p) d -> g p (s t) d", s=SEQS, p=P)

    with ExitStack() as ctx:
        def sb(name, shape, dt=F32):
            return ctx.enter_context(nc.sbuf_tensor(name, shape, dt))

        def sem(name):
            return ctx.enter_context(nc.semaphore(name))

        w13 = sb("w13", [P, NE, HID])
        w1hi, w1lo = sb("w1hi", [P, NE, HID], F32R), sb("w1lo", [P, NE, HID], F32R)
        w3hi, w3lo = sb("w3hi", [P, NE, HID], F32R), sb("w3lo", [P, NE, HID], F32R)
        w2s = sb("w2s", [P, NE, NH, D])
        wraw = sb("wraw", [P, 4, P])
        wqk = sb("wqk", [P, 2, P])
        wqkhi, wqklo = sb("wqkhi", [P, 2, P], F32R), sb("wqklo", [P, 2, P], F32R)
        wvr = sb("wvr", [P, P + E])
        woT = sb("woT", [P, P])
        bqk = sb("bqk", [P, 2])
        bv_b, bo_b = sb("bv_b", [P, P]), sb("bo_b", [P, P])
        ident, identb = sb("ident", [P, P]), sb("identb", [P, P], BF16)
        causal = sb("causal", [P, 4, P], BF16)
        onerow = sb("onerow", [P, 1])
        iota8 = sb("iota8", [P, E])
        minushalf = sb("minushalf", [P, NT])

        xin = [sb(f"xin{i}", [P, NT, D]) for i in range(2)]
        xres = [sb(f"xres{i}", [P, NT, D]) for i in range(2)]
        stats, mv = sb("stats", [P, NT, 6]), sb("mv", [P, NT, 2])
        vareps, rstd = sb("vareps", [P, NT]), sb("rstd", [P, NT])
        xn = sb("xn", [P, NT, D])
        xT = [sb(f"xT{i}", [P, T]) for i in range(2)]
        xThi = [sb(f"xThi{i}", [P, T], F32R) for i in range(2)]
        xTlo = [sb(f"xTlo{i}", [P, T], F32R) for i in range(2)]
        qkhi = [sb(f"qkhi{i}", [P, T], F32R) for i in range(2)]
        qklo = [sb(f"qklo{i}", [P, T], F32R) for i in range(2)]
        qst = sb("qst", [P, NG, T], F32R)
        qm = sb("qm", [P, NG, T], F32R)
        kbd = sb("kbd", [P, NG, NJ, T], F32R)
        va = [sb(f"va{i}", [P, NT, H, ROWS]) for i in range(2)]
        mx = sb("mx", [P, NG, NT, NJ])
        mcol = sb("mcol", [P, 2, NT, P])
        pt = sb("pt", [P, SLOTS, 2, 3 * P])
        oT = sb("oT", [P, NG, T])
        rec, on = sb("rec", [P, NT, H]), sb("on", [P, NT, D])
        onT = sb("onT", [P, T])
        lg = [sb(f"lg{i}", [P, NT, E]) for i in range(2)]
        top, topi, topf = sb("top", [P, NT, 8]), sb("topi", [P, NT, 8], U32), sb("topf", [P, NT, 8])
        gap, expgap, gden = sb("gap", [P, NT]), sb("expgap", [P, NT]), sb("gden", [P, NT])
        gate1, gate2 = sb("gate1", [P, NT]), sb("gate2", [P, NT])
        hot1, hot2 = sb("hot1", [P, NT, E]), sb("hot2", [P, NT, E])
        cw1, cw2, cw = sb("cw1", [P, NT, E]), sb("cw2", [P, NT, E]), sb("cw", [P, NT, E])
        act1 = [sb(f"act1_{i}", [P, T]) for i in range(2)]
        hid = [sb(f"hid{i}", [P, NH, T]) for i in range(2)]
        acc = sb("acc", [P, NT, D])
        res = [sb(f"res{i}", [P, NT, D]) for i in range(2)]

        A = [ctx.enter_context(nc.psum_tensor(f"A{i}", [P, 2, BANK], F32)) for i in range(2)]
        Y = [ctx.enter_context(nc.psum_tensor(f"Y{i}", [P, BANK], F32)) for i in range(2)]
        M = [ctx.enter_context(nc.psum_tensor(f"M{i}", [P, BANK], F32)) for i in range(2)]

        d_watt, d_wexp, d_w2, d_bias = sem("d_watt"), sem("d_wexp"), sem("d_w2"), sem("d_bias")
        c_pool, c_dve, c_ones = sem("c_pool"), sem("c_dve"), sem("c_ones")
        wT_ready, wT_copied = sem("wT_ready"), sem("wT_copied")
        wqk_hi, wqk_split = sem("wqk_hi"), sem("wqk_split")
        wexp_hi, wexp_split = sem("wexp_hi"), sem("wexp_split")
        waited = sem("waited")
        x_in = [sem(f"x_in{i}") for i in range(2)]
        stored = [sem(f"stored{i}") for i in range(2)]
        xres_done = sem("xres_done")
        stats_done = sem("stats_done")
        mv_done = sem("mv_done")
        var_done = sem("var_done")
        rstd_done = sem("rstd_done")
        xn_done = sem("xn_done")
        xT_full = sem("xT_full")
        xT_copied = sem("xT_copied")
        xT_hi = sem("xT_hi")
        xT_split = sem("xT_split")
        qk_full = sem("qk_full")
        qk_hi = sem("qk_hi")
        qk_split = sem("qk_split")
        qk_stacked = sem("qk_stacked")
        vr_full = sem("vr_full")
        v_copied = sem("v_copied")
        lg_copied = sem("lg_copied")
        routed = sem("routed")
        gap_exp = sem("gap_exp")
        qk_scores = sem("qk_scores")
        max_done = sem("max_done")
        m_split = sem("m_split")
        mT_full = sem("mT_full")
        qm_done = sem("qm_done")
        kq_scores = sem("kq_scores")
        exp_done = sem("exp_done")
        p_masked = sem("p_masked")
        o_full = sem("o_full")
        o_copied = sem("o_copied")
        oN_full = sem("oN_full")
        rec_done = sem("rec_done")
        on_done = sem("on_done")
        onT_full = sem("onT_full")
        onT_copied = sem("onT_copied")
        h1_full = sem("h1_full")
        h3_full = sem("h3_full")
        silu_done = sem("silu_done")
        hid_done = sem("hid_done")
        y_full = sem("y_full")
        y_added = sem("y_added")
        STACKS = 16 * 2 * NJ * 3
        ROUTE = 2 * NT + 9
        YADDS = E * NT + 1
        FIRST = 3

        USES = [("xT", 0), ("qk", 0), ("qk", 1), ("vr", 0), ("vr", 1)]
        USES += [("oN", t) for t in range(NT)] + [("onT", 0)]
        FINISH = set(USES[5:])
        for g in range(NG + 1):
            if g < NG:
                USES += [("scores", UNITS * g + k) for k in range(UNITS)]
            if g > 0:
                USES += [("mT", g - 1)]
        assert len(USES) % 2 == 0

        def bank(use):
            return M[USES.index(use) % 2]

        def freed(use, n, group):
            at = USES.index(use)
            before = [k for k in range(at % 2, at, 2) if (group if USES[k] in FINISH else n) is not None]
            if before:
                kind, k = USES[before[-1]]
                base = n if (kind, k) not in FINISH else group
            elif group is None:
                return None
            else:
                kind, k = USES[len(USES) - 2 + at % 2]
                base = group
            done, each = {"xT": (xT_hi, 1), "qk": (qk_split, 2), "vr": (lg_copied, 2), "oN": (on_done, NT),
                          "onT": (onT_copied, 1), "scores": (max_done, NG * UNITS), "mT": (qm_done, NG)}[kind]
            return done, base * each + k + 1

        def bank_free(pe, use, n, group):
            wait = freed(use, n, group)
            if wait:
                pe.wait_ge(*wait)

        def over_groups(eng, step):
            step(0, None, 1)
            with eng.Fori(0, GROUPS // 2 - 1) as i:
                step(i * 2 + 1, i * 2, 0)
                step(i * 2 + 2, i * 2 + 1, 1)
            step(GROUPS - 1, GROUPS - 2, 0)
            step(None, GROUPS - 1, 1)

        def x_count(n, par):
            return None if n is None else 8 * n + (8 if par else 16)

        block = ctx.enter_context(nc.Block())

        @block.sync
        def _(sp):
            for s in stored:
                sp.sem_inc(s, 16)
            for n, w in enumerate((wq, wk, wv, wo)):
                sp.dma_start(wraw[:, n, :], w).then_inc(d_watt, 16)
            sp.dma_start(xin[0][:], x_v[0]).then_inc(x_in[0], 16)
            sp.dma_start(xin[1][:], x_v[1]).then_inc(x_in[1], 16)
            sp.dma_start(wvr[:, P:P + E], w_router).then_inc(d_watt, 16)
            for n, b in enumerate((bq, bk)):
                for j in range(NJ):
                    sp.dma_start(bqk[ROWS * j:ROWS * j + ROWS, n:n + 1],
                                 b[ROWS * j:ROWS * j + ROWS].rearrange("(g d) -> d g", d=HD),
                                 allow_slow_non_contiguous=True).then_inc(d_bias, 16)
            for b, t in ((bv, bv_b), (bo, bo_b)):
                sp.dma_start(t[:], b.partition_broadcast(P)).then_inc(d_bias, 16)
            sp.dma_start(w13[:, 0:E, :], w1.rearrange("e d h -> d e h")).then_inc(d_wexp, 16)
            sp.dma_start(w13[:, E, :], sw1).then_inc(d_wexp, 16)
            for e in range(E):
                sp.dma_start(w2s[:, e], w2[e].rearrange("(a p) d -> p a d", p=P)).then_inc(d_w2, 16)
            sp.dma_start(w2s[:, E], sw2.rearrange("(a p) d -> p a d", p=P)).then_inc(d_w2, 16)

            def stack(n):
                for o, (dst, parts) in enumerate(((qst, (qkhi, qkhi, qklo)), (kbd, (qkhi, qklo, qkhi)))):
                    sp.wait_ge(qk_split, 2 * n + o + 1)
                    for j in range(NJ):
                        for r in range(3):
                            at = ROWS * j + HD * r
                            to = dst[at:at + HD] if o == 0 else dst[at:at + HD, :, j, :]
                            sp.dma_start(to.bitcast(F32), parts[r][o][ROWS * j:ROWS * j + ROWS, :].bitcast(F32)).then_inc(qk_stacked, 16)

            def step(n, group, par):
                if group is None:
                    sp.wait_ge(c_ones, NJ)
                    stack(n)
                    sp.wait_ge(wexp_split, 1)
                    sp.dma_start(w13[:, 0:E, :], w3.rearrange("e d h -> d e h")).then_inc(d_wexp, 16)
                    sp.dma_start(w13[:, E, :], sw3).then_inc(d_wexp, 16)
                    return
                if n is not None:
                    sp.wait_ge(kq_scores, PAIRS * (group + 1))
                    stack(n)
                if n is not None and not (isinstance(n, int) and n == GROUPS - 1):
                    sp.wait_ge(xn_done, NT * (group + 1))
                    sp.wait_ge(xres_done, group + 1)
                    sp.dma_start(xin[par][:], x_v[bass.ds(n + 1, 1)].rearrange("o p t d -> (o p) t d"))\
                      .then_inc(x_in[par], 16)
                sp.wait_ge(y_added, 1 + YADDS * (group + 1))
                sp.dma_start(out_v[bass.ds(group, 1)].rearrange("o p t d -> (o p) t d"), res[par][:])\
                  .then_inc(stored[par], 16)

            over_groups(sp, step)
            for s in stored:
                sp.wait_ge(s, 16 + 16 * GROUPS // 2)

        @block.gpsimd
        def _(pool):
            nc.gpsimd.memset(ident[:], 0.0).then_inc(c_pool, 1)
            nc.gpsimd.memset(identb[:], 0.0).then_inc(c_pool, 1)
            nc.gpsimd.memset(causal[:], 0.0).then_inc(c_pool, 1)
            pool.wait_ge(c_pool, 3)
            for m in (ident, identb):
                nc.gpsimd.affine_select(out=m[:], in_=m[:], compare_op=ALU.not_equal, fill=1.0, base=0,
                                        pattern=[[-1, P]], channel_multiplier=1).then_inc(c_pool, 1)
            nc.gpsimd.affine_select(out=causal[:], in_=causal[:], compare_op=ALU.is_ge, fill=MASKED, base=0,
                                    pattern=[[0, 4], [-1, P]], channel_multiplier=1).then_inc(c_pool, 1)
            nc.gpsimd.iota(iota8[:], pattern=[[1, E]], base=0, channel_multiplier=0,
                           allow_small_or_imprecise_dtypes=True).then_inc(c_pool, 1)
            nc.gpsimd.memset(minushalf[:], -0.5).then_inc(c_pool, 1)
            nc.gpsimd.memset(qst[:].bitcast(F32), 0.0).then_inc(c_pool, 1)
            nc.gpsimd.memset(kbd[:].bitcast(F32), 0.0).then_inc(c_pool, 1)
            nc.gpsimd.memset(mcol[:], 0.0).then_inc(c_pool, 1)
            pool.wait_ge(d_bias, 16 * (2 * NJ + 2))

            def xres_of(n, par, count):
                pool.wait_ge(x_in[par], count)
                nc.gpsimd.tensor_tensor(xres[par][:], xin[par][:],
                                        bo_b[:].unsqueeze(1).broadcast_to([P, NT, D]), ALU.add).then_inc(xres_done, 1)

            def inverse_deviation(n):
                pool.wait_ge(var_done, n + 1)
                nc.gpsimd.tensor_tensor(rstd[:], vareps[:], minushalf[:], ALU.pow).then_inc(rstd_done, 1)

            def split_x(n, par):
                pool.wait_ge(xT_hi, n + 1)
                nc.gpsimd.tensor_tensor(xTlo[par][:], xT[par][:], xThi[par][:].bitcast(F32),
                                        ALU.subtract).then_inc(xT_split, 1)

            def mask(group, p):
                pool.wait_ge(exp_done, PAIRS * group + p + 1)
                pool.sem_inc(waited)
                diag = pt[:, p % SLOTS, :, 0:2 * P]
                nc.gpsimd.affine_select(out=diag, in_=diag, compare_op=ALU.is_ge, fill=0.0, base=0,
                                        pattern=[[0, 2], [0, 2], [1, P]], channel_multiplier=-1).then_inc(p_masked, 1)

            def step(n, group, par):
                count = x_count(n, 1 - par)
                if group is None:
                    inverse_deviation(n)
                    xres_of(n, 1 - par, count)
                    split_x(n, 1 - par)
                    return
                for p in range(PAIRS):
                    if p == 0 and n is not None:
                        inverse_deviation(n)
                    mask(group, p)
                    if p == 5 and n is not None:
                        xres_of(n, 1 - par, count)
                    if p == 6 and n is not None:
                        split_x(n, 1 - par)

            over_groups(pool, step)

        @block.scalar
        def _(act):
            act.wait_ge(wT_copied, 2)
            nc.scalar.activation(wqkhi[:], wqk[:], ACT.Copy).then_inc(wqk_hi, 1)

            def split_x(n, par):
                act.wait_ge(xT_copied, n + 1)
                nc.scalar.activation(xThi[par][:], bank(("xT", 0))[:], ACT.Copy).then_inc(xT_hi, 1)

            def hi_of_qk(n):
                for o in range(2):
                    act.wait_ge(qk_full, 2 * n + o + 1)
                    if o == 0 and not (isinstance(n, int) and n == 0):
                        act.wait_ge(qk_stacked, STACKS * n)
                    nc.scalar.activation(qkhi[o][:], bank(("qk", o))[:], ACT.Identity,
                                         bias=bqk[:, o:o + 1]).then_inc(qk_hi, 1)

            def step(n, group, par):
                if group is None:
                    act.wait_ge(d_bias, 16 * (2 * NJ + 2))
                    split_x(n, 1 - par)
                    hi_of_qk(n)
                    for k, hi in enumerate((w1hi, w3hi)):
                        act.wait_ge(d_wexp, 32 * (k + 1))
                        nc.scalar.activation(hi[:], w13[:], ACT.Copy).then_inc(wexp_hi, 1)
                    return
                for p in range(PAIRS):
                    act.wait_ge(kq_scores, PAIRS * group + p + 1)
                    nc.scalar.activation(pt[:, p % SLOTS], A[p % 2][:, :, 0:3 * P], ACT.Exp, scale=SCALE)\
                      .then_inc(exp_done, 1)
                    if p == 2:
                        act.wait_ge(routed, ROUTE * group + 2 * NT + 2)
                        nc.scalar.activation(expgap[:], gap[:], ACT.Exp).then_inc(gap_exp, 1)
                    if p == 5 and n is not None:
                        split_x(n, 1 - par)
                    if p == 9 and n is not None:
                        hi_of_qk(n)
                    if p % 4 == 2 and p > 4:
                        copy_o(act, group, p // 4 - 1)
                copy_o(act, group, NG - 1)
                for s in range(STEPS):
                    act.wait_ge(h1_full, STEPS * group + s + 1)
                    nc.scalar.activation(act1[s % 2][:], A[s % 2][:, 0, :], ACT.Silu).then_inc(silu_done, 1)
                    if s == 3:
                        act.wait_ge(onT_full, group + 1)
                        nc.scalar.activation(onT[:], bank(("onT", 0))[:], ACT.Copy).then_inc(onT_copied, 1)

            def copy_o(act, group, g):
                act.wait_ge(o_full, NG * group + g + 1)
                nc.scalar.activation(oT[:, g, :], Y[g % 2][:], ACT.Copy).then_inc(o_copied, 1)

            over_groups(act, step)

        @block.vector
        def _(dve):
            dve.sem_inc(hid_done)
            dve.sem_inc(y_added)
            for i in range(2):
                nc.vector.memset(va[i][:], 0.0).then_inc(c_dve, 1)
            dve.wait_ge(c_dve, 2)
            for i in range(2):
                nc.vector.memset(va[i][:, :, :, HD:HD + 1], 1.0).then_inc(c_dve, 1)
            dve.wait_ge(c_pool, 11)
            nc.vector.tensor_reduce(onerow[:], ident[:].rearrange("p (j r) -> p j r", r=ROWS)[:, :, ONE:ONE + 2],
                                    AX.XY, ALU.add).then_inc(c_dve, 1)
            dve.wait_ge(wT_ready, 1)
            for o in range(2):
                nc.vector.tensor_copy(wqk[:, o, :].rearrange("p (j d g) -> p j g d", j=NJ, d=HD),
                                      A[0][:, 0, o * P:(o + 1) * P].rearrange("p (j g d) -> p j g d", j=NJ, d=HD))\
                  .then_inc(wT_copied, 1)
            nc.vector.tensor_copy(wvr[:, 0:P], A[0][:, 0, 2 * P:3 * P]).then_inc(wT_copied, 1)
            nc.vector.tensor_copy(woT[:], A[0][:, 0, 3 * P:4 * P]).then_inc(wT_copied, 1)
            dve.wait_ge(wqk_hi, 1)
            nc.vector.tensor_tensor(wqklo[:], wqk[:], wqkhi[:].bitcast(F32), ALU.subtract).then_inc(wqk_split, 1)
            dve.wait_ge(c_dve, 5)
            for j in range(NJ):
                rows = slice(ROWS * j, ROWS * (j + 1))
                nc.vector.tensor_scalar(kbd[rows, :, j, :], kbd[rows, :, j, :].bitcast(F32), onerow[rows, 0:1], None,
                                        ALU.add).then_inc(c_ones, 1)

            def norm_stats(n, par, count):
                dve.wait_ge(x_in[par], count)
                for t in range(NT):
                    nc.vector.bn_stats(stats[:, t, :], xin[par][:, t, :]).then_inc(stats_done, 1)
                dve.wait_ge(stats_done, NT * (n + 1))
                dve.sem_inc(waited)
                for t in range(NT):
                    nc.vector.bn_aggr(mv[:, t, :], stats[:, t, :]).then_inc(mv_done, 1)
                dve.wait_ge(mv_done, NT * (n + 1))
                nc.vector.tensor_scalar(vareps[:], mv[:, :, 1], EPS, None, ALU.add).then_inc(var_done, 1)

            def norm_apply(n, par):
                dve.wait_ge(rstd_done, n + 1)
                for t in range(NT):
                    nc.vector.tensor_scalar(xn[:, t, :], xin[par][:, t, :], mv[:, t, 0:1], rstd[:, t:t + 1],
                                            ALU.subtract, ALU.mult).then_inc(xn_done, 1)

            def copy_x(n, par):
                dve.wait_ge(xT_full, n + 1)
                nc.vector.tensor_copy(xT[par][:], bank(("xT", 0))[:]).then_inc(xT_copied, 1)

            def lo_of_qk(n, o):
                dve.wait_ge(qk_hi, 2 * n + o + 1)
                nc.vector.scalar_tensor_tensor(out=qklo[o][:], in0=bank(("qk", o))[:], scalar=bqk[:, o:o + 1],
                                               in1=qkhi[o][:].bitcast(F32), op0=ALU.add, op1=ALU.subtract)\
                  .then_inc(qk_split, 1)

            def copy_v(n, par, k):
                dve.wait_ge(vr_full, 2 * n + k + 1)
                src = bank(("vr", k))[:, 0:2 * (P + E)].rearrange("p (t c) -> p t c", t=2)
                for t in range(2):
                    last = nc.vector.tensor_tensor(va[par][:, 2 * k + t, :, 0:HD],
                                                   src[:, t, 0:P].rearrange("p (h d) -> p h d", d=HD),
                                                   bv_b[:].rearrange("p (h d) -> p h d", d=HD), ALU.add)
                last.then_inc(v_copied, 1)
                nc.vector.tensor_copy(lg[par][:, 2 * k:2 * k + 2, :], src[:, :, P:P + E]).then_inc(lg_copied, 1)

            def route_top(group, par):
                dve.wait_ge(lg_copied, 2 * (group + 1))
                dve.sem_inc(waited)
                for t in range(NT):
                    nc.vector.max(top[:, t, :], lg[par][:, t, :]).then_inc(routed, 1)
                dve.wait_ge(routed, ROUTE * group + NT)
                dve.sem_inc(waited)
                for t in range(NT):
                    nc.vector.max_index(topi[:, t, :], top[:, t, :], lg[par][:, t, :]).then_inc(routed, 1)
                dve.wait_ge(routed, ROUTE * group + 2 * NT)
                nc.vector.tensor_copy(topf[:], topi[:]).then_inc(routed, 1)
                nc.vector.tensor_tensor(gap[:], top[:, :, 1], top[:, :, 0], ALU.subtract).then_inc(routed, 1)

            def route_gates(group):
                k = ROUTE * group + 2 * NT + 2
                dve.wait_ge(routed, k)
                for hot, which in ((hot1, 0), (hot2, 1)):
                    nc.vector.tensor_tensor(hot[:], iota8[:].unsqueeze(1).broadcast_to([P, NT, E]),
                                            topf[:, :, which:which + 1].broadcast_to([P, NT, E]),
                                            ALU.is_equal).then_inc(routed, 1)
                dve.wait_ge(gap_exp, group + 1)
                nc.vector.tensor_scalar(gden[:], expgap[:], 1.0, None, ALU.add).then_inc(routed, 1)
                dve.wait_ge(routed, k + 3)
                nc.vector.reciprocal(gate1[:], gden[:]).then_inc(routed, 1)
                dve.wait_ge(routed, k + 4)
                nc.vector.tensor_tensor(cw1[:], hot1[:], gate1[:].unsqueeze(2).broadcast_to([P, NT, E]),
                                        ALU.mult)
                nc.vector.tensor_tensor(gate2[:], expgap[:], gate1[:], ALU.mult).then_inc(routed, 1)
                dve.wait_ge(routed, k + 5)
                nc.vector.tensor_tensor(cw2[:], hot2[:], gate2[:].unsqueeze(2).broadcast_to([P, NT, E]),
                                        ALU.mult).then_inc(routed, 1)
                dve.wait_ge(routed, k + 6)
                nc.vector.tensor_tensor(cw[:], cw1[:], cw2[:], ALU.add).then_inc(routed, 1)

            def maxima(n, g):
                for k in range(UNITS):
                    b, u = divmod(k, 3)
                    src = bank(("scores", UNITS * g + k))
                    dve.wait_ge(qk_scores, UNITS * (NG * n + g) + k + 1)
                    if u == 0:
                        o, i = mx[:, g, QT * b, :], src[:].rearrange("p (j k) -> p j k", j=NJ)
                    else:
                        o, i = mx[:, g, QT * b + 1, 2 * u - 2:2 * u], src[:].rearrange("p (j k) -> p j k", j=2)
                    nc.vector.reduce_max(o, i, AX.X).then_inc(max_done, 1)
                cols = mcol[:, g % 2].rearrange("p t (j r) -> p t j r", r=ROWS)
                dve.wait_ge(max_done, UNITS * (NG * n + g + 1))
                nc.vector.tensor_scalar(cols[:, :, :, ONE].bitcast(F32R), mx[:, g], -1.0, None,
                                        ALU.mult).then_inc(m_split, 1)
                dve.wait_ge(m_split, 2 * (NG * n + g) + 1)
                nc.vector.scalar_tensor_tensor(out=cols[:, :, :, ONE + 1].bitcast(F32R), in0=mx[:, g], scalar=-1.0,
                                               in1=cols[:, :, :, ONE], op0=ALU.mult,
                                               op1=ALU.subtract).then_inc(m_split, 1)

            def add_max(n, g):
                dve.wait_ge(mT_full, NG * n + g + 1)
                nc.vector.tensor_tensor(qm[:, g, :], qst[:, g, :].bitcast(F32), bank(("mT", g))[:],
                                        ALU.add).then_inc(qm_done, 1)

            def normalise(group, t):
                src = bank(("oN", t))[:].rearrange("p (g j r) -> p g j r", g=NG, r=ROWS)
                dve.wait_ge(oN_full, NT * group + t + 1)
                r = rec[:, t, :].rearrange("p (g j) -> p g j", j=NJ)
                nc.vector.reciprocal(r, src[:, :, :, HD]).then_inc(rec_done, 1)
                dve.wait_ge(rec_done, NT * group + t + 1)
                nc.vector.tensor_tensor(on[:, t, :].rearrange("p (j g d) -> p g j d", g=NG, d=HD), src[:, :, :, 0:HD],
                                        r.unsqueeze(3).broadcast_to([P, NG, NJ, HD]), ALU.mult).then_inc(on_done, 1)

            def hidden(group, s):
                dve.wait_ge(h3_full, STEPS * group + s + 1)
                dve.wait_ge(silu_done, STEPS * group + s + 1)
                nc.vector.tensor_tensor(hid[s // NH % 2][:, s % NH, :], act1[s % 2][:], A[s % 2][:, 1, :],
                                        ALU.mult).then_inc(hid_done, 1)

            def add_expert(group, par, e):
                dve.wait_ge(y_full, NE * group + e + 1)
                if e == 0:
                    dve.wait_ge(xres_done, group + 1)
                if e < E:
                    for t in range(NT):
                        if e > 0:
                            dve.wait_ge(y_added, 1 + YADDS * group + NT * (e - 1) + t + 1)
                        before = xres[par] if e == 0 else acc
                        nc.vector.scalar_tensor_tensor(out=acc[:, t, :], in0=Y[e % 2][:, t * D:(t + 1) * D],
                                                       scalar=cw[:, t, e:e + 1], in1=before[:, t, :],
                                                       op0=ALU.mult, op1=ALU.add).then_inc(y_added, 1)
                else:
                    dve.wait_ge(y_added, 1 + YADDS * group + NT * E)
                    dve.wait_ge(stored[par], 16 + 8 * group - (8 if par else 0))
                    nc.vector.tensor_tensor(res[par][:], acc[:], Y[e % 2][:].rearrange("p (t d) -> p t d", d=D),
                                            ALU.add).then_inc(y_added, 1)

            def step(n, group, par):
                count = x_count(n, 1 - par)
                if n is not None:
                    norm_stats(n, 1 - par, count)
                if group is not None:
                    route_top(group, par)
                if n is not None:
                    norm_apply(n, 1 - par)
                if group is not None:
                    route_gates(group)
                if n is not None:
                    if group is None:
                        dve.wait_ge(d_bias, 16 * (2 * NJ + 2))
                    copy_x(n, 1 - par)
                    lo_of_qk(n, 0)
                    lo_of_qk(n, 1)
                    copy_v(n, 1 - par, 0)
                    copy_v(n, 1 - par, 1)
                if group is None:
                    for g in range(NG):
                        maxima(n, g)
                        if g > 0:
                            add_max(n, g - 1)
                    add_max(n, NG - 1)
                    for k, (hi, lo) in enumerate(((w1hi, w1lo), (w3hi, w3lo))):
                        dve.wait_ge(wexp_hi, k + 1)
                        nc.vector.tensor_tensor(lo[:], w13[:], hi[:].bitcast(F32), ALU.subtract).then_inc(wexp_split, 1)
                    return
                for e in range(NE):
                    hidden(group, NH * e)
                    hidden(group, NH * e + 1)
                    if e > 0:
                        add_expert(group, par, e - 1)
                    if e == 0:
                        for t in range(NT):
                            normalise(group, t)
                    if n is not None and FIRST <= e <= FIRST + NG:
                        g = e - FIRST
                        if g < NG:
                            maxima(n, g)
                        if g > 0:
                            add_max(n, g - 1)
                add_expert(group, par, NE - 1)

            over_groups(dve, step)

        @block.tensor
        def _(pe):
            pe.wait_ge(c_pool, 11)
            pe.wait_ge(d_watt, 16 * 5)
            for k in range(4):
                last = nc.tensor.transpose(A[0][:, 0, k * P:(k + 1) * P], wraw[:, k, :], ident[:])
            last.then_inc(wT_ready, 1)

            def three(o, hi, lo, xhi, xlo):
                nc.tensor.matmul(o, hi, xhi, start=True, stop=False)
                nc.tensor.matmul(o, hi, xlo, start=False, stop=False)
                return nc.tensor.matmul(o, lo, xhi, start=False, stop=True)

            def transpose_x(n, group):
                bank_free(pe, ("xT", 0), n, group)
                pe.wait_ge(xn_done, NT * (n + 1))
                for t in range(NT):
                    last = nc.tensor.transpose(bank(("xT", 0))[:, t * P:(t + 1) * P], xn[:, t, :], ident[:])
                last.then_inc(xT_full, 1)

            def project_qk(n, group, par):
                pe.wait_ge(xT_split, n + 1)
                for o in range(2):
                    bank_free(pe, ("qk", o), n, group)
                    three(bank(("qk", o))[:], wqkhi[:, o, :], wqklo[:, o, :], xThi[par][:], xTlo[par][:])\
                        .then_inc(qk_full, 1)

            def project_v(n, group, par):
                for k in range(2):
                    bank_free(pe, ("vr", k), n, group)
                    for t in range(2):
                        last = nc.tensor.matmul(bank(("vr", k))[:, t * (P + E):(t + 1) * (P + E)],
                                                xT[par][:, (2 * k + t) * P:(2 * k + t + 1) * P], wvr[:],
                                                start=True, stop=True)
                    last.then_inc(vr_full, 1)

            def scores(n, group, g):
                if g == 0:
                    pe.wait_ge(qk_stacked, STACKS * (n + 1))
                for k in range(UNITS):
                    b, u = divmod(k, 3)
                    use = ("scores", UNITS * g + k)
                    o = bank(use)
                    bank_free(pe, use, n, group)
                    at = b * S + (P if u else 0)
                    q = qst[:, g, at:at + P]
                    if u == 0:
                        nc.tensor.matmul(o[:].rearrange("p (j k) -> p j k", j=NJ), q, kbd[:, g, :, at:at + P],
                                         start=True, stop=False)
                        last = nc.tensor.matmul(o[:].rearrange("p (j k) -> p j k", j=NJ), identb[:], causal[:],
                                                start=False, stop=True)
                    else:
                        nc.tensor.matmul(o[:].rearrange("p (j k) -> p j k", j=2), q,
                                         kbd[:, g, 2 * u - 2:2 * u, b * S:(b + 1) * S], start=True, stop=False)
                        last = nc.tensor.matmul(o[:].rearrange("p (j k) -> p j k", j=2)[:, :, P:2 * P], identb[:],
                                                causal[:, 0:2, :], start=False, stop=True)
                    last.then_inc(qk_scores, 1)

            def transpose_max(n, group, g):
                bank_free(pe, ("mT", g), n, group)
                pe.wait_ge(m_split, 2 * (NG * n + g + 1))
                for t in range(NT):
                    last = nc.tensor.transpose(bank(("mT", g))[:, t * P:(t + 1) * P], mcol[:, g % 2, t, :], ident[:])
                last.then_inc(mT_full, 1)

            def of_pair(p):
                g, r = divmod(p, SEQS * 2)
                return g, r // 2, (r % 2) * 2

            def pair_scores(group, p):
                g, b, j0 = of_pair(p)
                if p == 0:
                    pe.wait_ge(hid_done, 1 + STEPS * group)
                if p % 4 == 0:
                    pe.wait_ge(qm_done, NG * group + g + 1)
                if p >= 2:
                    pe.wait_ge(exp_done, PAIRS * group + p - 1)
                for a in range(2):
                    o = A[p % 2][:, a, 0:3 * P].rearrange("p (c q) -> p c q", q=P)
                    for kt, columns in ((1, o[:, 0:2]), (0, o[:, 0:3:2])):
                        last = nc.tensor.matmul(columns, kbd[:, g, j0 + a, b * S + kt * P:b * S + (kt + 1) * P],
                                                qm[:, g, b * S:(b + 1) * S].rearrange("p (c q) -> p c q", q=P),
                                                start=True, stop=True)
                last.then_inc(kq_scores, 1)

            def pair_output(group, par, p):
                g, b, j0 = of_pair(p)
                if p == 0:
                    pe.wait_ge(v_copied, 2 * (group + 1))
                    pe.wait_ge(y_added, 1 + YADDS * group)
                if p % 4 == 0 and g >= 2:
                    pe.wait_ge(o_copied, NG * group + g - 1)
                pe.wait_ge(p_masked, PAIRS * group + p + 1)
                for a in range(2):
                    j = j0 + a
                    o = Y[g % 2][ROWS * j:ROWS * (j + 1), b * S:(b + 1) * S]
                    h = NG * j + g
                    pr = pt[:, p % SLOTS, a, :].rearrange("p (c q) -> p c q", q=P)
                    nc.tensor.matmul(o.rearrange("p (c q) -> p c q", q=P), va[par][:, QT * b, h, :], pr[:, 0:3:2],
                                     start=True, stop=False)
                    last = nc.tensor.matmul(o[:, P:2 * P], va[par][:, QT * b + 1, h, :], pr[:, 1],
                                            start=False, stop=True)
                if p % 4 == 3:
                    last.then_inc(o_full, 1)

            def up(group, par, e):
                for hh in range(NH):
                    s = NH * e + hh
                    if s < 2:
                        pe.wait_ge(exp_done, PAIRS * (group + 1) - 1 + s)
                    else:
                        pe.wait_ge(hid_done, STEPS * group + s)
                    c = slice(hh * P, (hh + 1) * P)
                    three(A[s % 2][:, 0, :], w1hi[:, e, c], w1lo[:, e, c], xThi[par][:], xTlo[par][:])\
                        .then_inc(h1_full, 1)
                    three(A[s % 2][:, 1, :], w3hi[:, e, c], w3lo[:, e, c], xThi[par][:], xTlo[par][:])\
                        .then_inc(h3_full, 1)

            def down(group, e):
                if e < 2:
                    pe.wait_ge(o_copied, NG * (group + 1) - 1 + e)
                else:
                    pe.wait_ge(y_added, 1 + YADDS * group + NT * (e - 1))
                pe.wait_ge(hid_done, 1 + STEPS * group + NH * (e + 1))
                if e == NE - 1:
                    pe.wait_ge(onT_copied, group + 1)
                for t in range(NT):
                    o, c = Y[e % 2][:, t * D:(t + 1) * D], slice(t * P, (t + 1) * P)
                    for hh in range(NH):
                        last = nc.tensor.matmul(o, hid[e % 2][:, hh, c], w2s[:, e, hh, :], start=(hh == 0),
                                                stop=(hh == NH - 1 and e < NE - 1))
                    if e == NE - 1:
                        last = nc.tensor.matmul(o, onT[:, c], woT[:], start=False, stop=True)
                last.then_inc(y_full, 1)

            def attention_rows(n, group):
                for t in range(NT):
                    bank_free(pe, ("oN", t), n, group)
                    pe.wait_ge(o_copied, NG * (group + 1))
                    for g in range(NG):
                        last = nc.tensor.transpose(bank(("oN", t))[:, g * P:(g + 1) * P], oT[:, g, t * P:(t + 1) * P],
                                                   ident[:])
                    last.then_inc(oN_full, 1)

            def attention_columns(n, group):
                bank_free(pe, ("onT", 0), n, group)
                pe.wait_ge(on_done, NT * (group + 1))
                for t in range(NT):
                    last = nc.tensor.transpose(bank(("onT", 0))[:, t * P:(t + 1) * P], on[:, t, :], ident[:])
                last.then_inc(onT_full, 1)

            def step(n, group, par):
                if group is None:
                    transpose_x(n, group)
                    pe.wait_ge(wqk_split, 1)
                    project_qk(n, group, 1 - par)
                    pe.wait_ge(wT_copied, 4)
                    project_v(n, group, 1 - par)
                    for g in range(NG):
                        scores(n, group, g)
                        if g > 0:
                            transpose_max(n, group, g - 1)
                    transpose_max(n, group, NG - 1)
                    pe.wait_ge(wexp_split, 2)
                    pe.wait_ge(d_w2, 16 * NE)
                    pe.wait_ge(c_dve, 4)
                    return
                lag = 3
                for p in range(PAIRS + lag):
                    if p < PAIRS:
                        pair_scores(group, p)
                    if n is not None:
                        if p == 4:
                            transpose_x(n, group)
                        if p == 8:
                            project_qk(n, group, 1 - par)
                        if p == 10:
                            project_v(n, group, 1 - par)
                    if p >= lag:
                        pair_output(group, par, p - lag)
                for e in range(NE):
                    up(group, par, e)
                    if e > 0:
                        down(group, e - 1)
                    if e == 0:
                        attention_rows(n, group)
                    if e == 1:
                        attention_columns(n, group)
                    if n is not None and FIRST <= e <= FIRST + NG:
                        g = e - FIRST
                        if g < NG:
                            scores(n, group, g)
                        if g > 0:
                            transpose_max(n, group, g - 1)
                down(group, NE - 1)

            over_groups(pe, step)


_INS = ["L0_attn_x", "L0_attn_Wq", "L0_attn_bq", "L0_attn_Wk", "L0_attn_bk", "L0_attn_Wv", "L0_attn_bv", "L0_attn_Wo",
        "L0_attn_bo", "L0_ffn_w_router", "L0_ffn_w1", "L0_ffn_w3", "L0_ffn_w2", "L0_ffn_sw1", "L0_ffn_sw3",
        "L0_ffn_sw2"]


def kernel(**inputs):
    import numpy as _np
    import concourse.bacc as _bacc
    from concourse.bass_utils import run_bass_kernel_spmd as _run

    nc = _bacc.Bacc("TRN2", target_bir_lowering=False, num_devices=1)
    arrays, args = {}, []
    for name in _INS:
        a = _np.ascontiguousarray(inputs[name])
        arrays[f"in_{name}"] = a
        args.append(nc.dram_tensor(f"in_{name}", a.shape, mybir.dt.from_np(a.dtype), kind="ExternalInput").ap())
    shape = arrays["in_L0_attn_x"].shape
    args.append(nc.dram_tensor("out_0", shape, F32, kind="ExternalOutput").ap())
    program(nc, *args)
    r = _run(nc, [arrays], core_ids=[0])
    return r.results[0]["out_0"]
```

```python
from contextlib import ExitStack

import concourse.bass as bass
from concourse import mybir

F32 = mybir.dt.float32
F32R = mybir.dt.float32r
U32 = mybir.dt.uint32
ALU = mybir.AluOpType
ACT = mybir.ActivationFunctionType
AX = mybir.AxisListType

P = 128
BANK = 512
NJ = 4
ROWS = P // NJ
EPS = 1e-5
MASKED = -3.0e38


def program(nc, x, wq, bq, wk, bk, wv, bv, wo, bo, w_router, w1, w3, w2, sw1, sw3, sw2, out):
    B, S, D = x.shape
    E, _, HID = w1.shape
    HD = 8
    H = D // HD
    NG = H // NJ
    SEQS = 2
    T = SEQS * S
    NT = T // P
    QT = S // P
    GROUPS = B // SEQS
    NE = E + 1
    NH = HID // P
    STEPS = NE * NH
    PAIRS = NG * SEQS * NJ // 2
    UNITS = SEQS * 3
    SLOTS = 4
    RING = 4
    SCALE = float(HD) ** -0.5
    ONE = 3 * NJ * HD
    ROWS_M = 2 * NJ
    assert D == P and T == BANK and QT == 2 and NH == 2 and GROUPS % 2 == 0 and E == 8

    x_v = x.rearrange("(g s) (t p) d -> g p (s t) d", s=SEQS, p=P)
    out_v = out.rearrange("(g s) (t p) d -> g p (s t) d", s=SEQS, p=P)

    with ExitStack() as ctx:
        def sb(name, shape, dt=F32):
            return ctx.enter_context(nc.sbuf_tensor(name, shape, dt))

        def sem(name):
            return ctx.enter_context(nc.semaphore(name))

        w1hi, w1lo = sb("w1hi", [P, NE, HID], F32R), sb("w1lo", [P, NE, HID], F32R)
        w3hi, w3lo = sb("w3hi", [P, NE, HID], F32R), sb("w3lo", [P, NE, HID], F32R)
        w2s = sb("w2s", [P, NE, NH, D])
        wraw = sb("wraw", [P, 4, P])
        wqk = sb("wqk", [P, 2, P])
        wqkhi, wqklo = sb("wqkhi", [P, 2, P], F32R), sb("wqklo", [P, 2, P], F32R)
        wvr = sb("wvr", [P, P + E])
        woT = sb("woT", [P, P])
        bqk = sb("bqk", [P, 2])
        bv_b, bo_b = sb("bv_b", [P, P]), sb("bo_b", [P, P])
        ident = sb("ident", [P, P])
        onecol = sb("onecol", [P, NJ])
        iota8 = sb("iota8", [P, E])
        minushalf = sb("minushalf", [P, NT])

        xin = [sb(f"xin{i}", [P, NT, D]) for i in range(2)]
        xres = [sb(f"xres{i}", [P, NT, D]) for i in range(2)]
        stats, mv = sb("stats", [P, NT, 6]), sb("mv", [P, NT, 2])
        vareps, rstd = sb("vareps", [P, NT]), sb("rstd", [P, NT])
        xn = sb("xn", [P, NT, D])
        xT = [sb(f"xT{i}", [P, T]) for i in range(2)]
        xThi = [sb(f"xThi{i}", [P, T], F32R) for i in range(2)]
        xTlo = [sb(f"xTlo{i}", [P, T], F32R) for i in range(2)]
        qkhi = [sb(f"qkhi{i}", [P, T], F32R) for i in range(2)]
        qklo = [sb(f"qklo{i}", [P, T], F32R) for i in range(2)]
        qst = [sb(f"qst{i}", [P, NG, T], F32R) for i in range(2)]
        kbd = sb("kbd", [P, NJ, NG, T], F32R)
        va = [sb(f"va{i}", [P, NT, H, ROWS]) for i in range(2)]
        sc = sb("sc", [P, RING, BANK])
        mx = sb("mx", [P, NG, NT, NJ])
        mcol = sb("mcol", [P, 2, NT, NJ, 2])
        pt = sb("pt", [P, SLOTS, 2, 3 * P])
        oT = sb("oT", [P, NG, T])
        rec, on = sb("rec", [P, NT, H]), sb("on", [P, NT, D])
        onT = sb("onT", [P, T])
        lg = [sb(f"lg{i}", [P, NT, E]) for i in range(2)]
        top, topi, topf = sb("top", [P, NT, 8]), sb("topi", [P, NT, 8], U32), sb("topf", [P, NT, 8])
        gap, expgap, gden = sb("gap", [P, NT]), sb("expgap", [P, NT]), sb("gden", [P, NT])
        gate1, gate2 = sb("gate1", [P, NT]), sb("gate2", [P, NT])
        hot1, hot2 = sb("hot1", [P, NT, E]), sb("hot2", [P, NT, E])
        cw1, cw2, cw = sb("cw1", [P, NT, E]), sb("cw2", [P, NT, E]), sb("cw", [P, NT, E])
        act1 = [sb(f"act1_{i}", [P, T]) for i in range(2)]
        hid = [sb(f"hid{i}", [P, NH, T]) for i in range(2)]
        acc = sb("acc", [P, NT, D])
        res = [sb(f"res{i}", [P, NT, D]) for i in range(2)]

        w1raw = pt[:].rearrange("p s a c -> p (s a c)")[:, 0:NE * HID].rearrange("p (e h) -> p e h", h=HID)
        w3raw = w2s[:].rearrange("p e a d -> p e (a d)")

        A = [ctx.enter_context(nc.psum_tensor(f"A{i}", [P, 2, BANK], F32)) for i in range(2)]
        Y = [ctx.enter_context(nc.psum_tensor(f"Y{i}", [P, BANK], F32)) for i in range(2)]
        M = [ctx.enter_context(nc.psum_tensor(f"M{i}", [P, BANK], F32)) for i in range(2)]

        d_watt, d_w1, d_w3, d_w2, d_bias = sem("d_watt"), sem("d_w1"), sem("d_w3"), sem("d_w2"), sem("d_bias")
        c_ident, c_small, c_kzero = sem("c_ident"), sem("c_small"), sem("c_kzero")
        c_va, c_onecol = sem("c_va"), sem("c_onecol")
        wT_ready, wT_copied = sem("wT_ready"), sem("wT_copied")
        wqk_hi, wqk_split = sem("wqk_hi"), sem("wqk_split")
        wexp_hi, wexp_split = sem("wexp_hi"), sem("wexp_split")
        waited = sem("waited")
        x_in = [sem(f"x_in{i}") for i in range(2)]
        stored = [sem(f"stored{i}") for i in range(2)]
        xres_done = sem("xres_done")
        stats_done = sem("stats_done")
        mv_done = sem("mv_done")
        var_done = sem("var_done")
        rstd_done = sem("rstd_done")
        xn_done = sem("xn_done")
        xT_full = sem("xT_full")
        xT_copied = sem("xT_copied")
        xT_hi = sem("xT_hi")
        xT_split = sem("xT_split")
        qk_full = sem("qk_full")
        qk_hi = sem("qk_hi")
        qk_split = sem("qk_split")
        qk_stacked = sem("qk_stacked")
        vr_full = sem("vr_full")
        v_copied = sem("v_copied")
        lg_copied = sem("lg_copied")
        routed = sem("routed")
        gap_exp = sem("gap_exp")
        qk_scores = sem("qk_scores")
        sc_copied = sem("sc_copied")
        sc_masked = sem("sc_masked")
        max_done = sem("max_done")
        m_split = sem("m_split")
        mT_full = sem("mT_full")
        m_rows = sem("m_rows")
        kq_scores = sem("kq_scores")
        exp_done = sem("exp_done")
        p_masked = sem("p_masked")
        o_full = sem("o_full")
        o_copied = sem("o_copied")
        oN_full = sem("oN_full")
        rec_done = sem("rec_done")
        on_done = sem("on_done")
        onT_full = sem("onT_full")
        onT_copied = sem("onT_copied")
        h1_full = sem("h1_full")
        h3_full = sem("h3_full")
        silu_done = sem("silu_done")
        hid_done = sem("hid_done")
        y_full = sem("y_full")
        y_added = sem("y_added")
        STACKS = 16 * (3 + 3 * NJ)
        ROUTE = 2 * NT + 9
        YADDS = E * NT + 1
        PER_SLOT = 2
        EARLY = 2
        X_AT, V_AT, QK_AT = 2, 4, 7
        FIRST = 4
        SLOTS_G = UNITS // PER_SLOT
        ROWS_AT = 2
        MAX_SLOTS = NG * SLOTS_G + ROWS_AT + 1

        USES = [("xT", 0), ("vr", 0), ("vr", 1), ("qk", 0), ("qk", 1)]
        USES += [("oN", t) for t in range(NT)] + [("onT", 0)]
        FINISH = set(USES[5:])
        for slot in range(MAX_SLOTS):
            g, k = divmod(slot, SLOTS_G)
            if g > 0 and k == ROWS_AT:
                USES += [("mT", g - 1)]
            if g < NG:
                USES += [("scores", PER_SLOT * slot + u) for u in range(PER_SLOT)]
        assert STEPS - FIRST == MAX_SLOTS - 1
        assert len(USES) % 2 == 0

        def bank(use):
            return M[USES.index(use) % 2]

        def freed(use, n, group):
            at = USES.index(use)
            before = [k for k in range(at % 2, at, 2) if (group if USES[k] in FINISH else n) is not None]
            if before:
                kind, k = USES[before[-1]]
                base = n if (kind, k) not in FINISH else group
            elif group is None:
                return None
            else:
                kind, k = USES[len(USES) - 2 + at % 2]
                base = group
            done, each = {"xT": (xT_hi, 1), "qk": (qk_split, 2), "vr": (lg_copied, 2), "oN": (on_done, NT),
                          "onT": (onT_copied, 1), "scores": (sc_copied, NG * UNITS), "mT": (m_rows, NG)}[kind]
            return done, base * each + k + 1

        def bank_free(pe, use, n, group):
            wait = freed(use, n, group)
            if wait:
                pe.wait_ge(*wait)

        def over_groups(eng, step):
            step(0, None, 1)
            with eng.Fori(0, GROUPS // 2 - 1) as i:
                step(i * 2 + 1, i * 2, 0)
                step(i * 2 + 2, i * 2 + 1, 1)
            step(GROUPS - 1, GROUPS - 2, 0)
            step(None, GROUPS - 1, 1)

        def has_next(n):
            return n is not None and not (isinstance(n, int) and n == GROUPS - 1)

        def x_count(n, par):
            return None if n is None else 8 * n + (8 if par else 16)

        block = ctx.enter_context(nc.Block())

        @block.sync
        def _(sp):
            for s in stored:
                sp.sem_inc(s, 16)
            sp.dma_start(xin[0][:], x_v[0]).then_inc(x_in[0], 16)
            for n, w in enumerate((wq, wk, wv, wo)):
                sp.dma_start(wraw[:, n, :], w).then_inc(d_watt, 16)
            sp.dma_start(wvr[:, P:P + E], w_router).then_inc(d_watt, 16)
            for n, b in enumerate((bq, bk)):
                for j in range(NJ):
                    sp.dma_start(bqk[ROWS * j:ROWS * j + ROWS, n:n + 1],
                                 b[ROWS * j:ROWS * j + ROWS].rearrange("(g d) -> d g", d=HD),
                                 allow_slow_non_contiguous=True).then_inc(d_bias, 16)
            for b, t in ((bv, bv_b), (bo, bo_b)):
                sp.dma_start(t[:], b.partition_broadcast(P)).then_inc(d_bias, 16)
            for raw, w, sw, there in ((w1raw, w1, sw1, d_w1), (w3raw, w3, sw3, d_w3)):
                sp.dma_start(raw[:, 0:E, :], w.rearrange("e d h -> d e h")).then_inc(there, 16)
                sp.dma_start(raw[:, E, :], sw).then_inc(there, 16)
            sp.dma_start(xin[1][:], x_v[1]).then_inc(x_in[1], 16)

            def stack_q(n, par):
                sp.wait_ge(qk_split, 2 * n + 1)
                for r, part in enumerate((qkhi[0], qkhi[0], qklo[0])):
                    sp.dma_start(qst[par][NJ * HD * r:NJ * HD * (r + 1)].bitcast(F32), part[:].bitcast(F32))\
                      .then_inc(qk_stacked, 16)

            def stack_k(n, group):
                sp.wait_ge(qk_split, 2 * n + 2)
                sp.sem_inc(waited)
                if group is None:
                    sp.wait_ge(c_kzero, 1 + NJ)
                else:
                    sp.wait_ge(kq_scores, PAIRS * (group + 1))
                for r, part in enumerate((qkhi[1], qklo[1], qkhi[1])):
                    for j in range(NJ):
                        at = HD * (NJ * r + j)
                        sp.dma_start(kbd[at:at + HD, j].bitcast(F32), part[ROWS * j:ROWS * (j + 1), :].bitcast(F32))\
                          .then_inc(qk_stacked, 16)

            def step(n, group, par):
                if group is None:
                    stack_q(n, 1 - par)
                    stack_k(n, group)
                    sp.wait_ge(wexp_split, 2)
                    for e in range(E):
                        sp.dma_start(w2s[:, e], w2[e].rearrange("(a p) d -> p a d", p=P)).then_inc(d_w2, 16)
                    sp.dma_start(w2s[:, E], sw2.rearrange("(a p) d -> p a d", p=P)).then_inc(d_w2, 16)
                    return
                if has_next(n):
                    sp.wait_ge(xn_done, NT * (group + 1))
                    sp.wait_ge(xres_done, group + 1)
                    sp.dma_start(xin[par][:], x_v[bass.ds(n + 1, 1)].rearrange("o p t d -> (o p) t d"))\
                      .then_inc(x_in[par], 16)
                if n is not None:
                    stack_q(n, 1 - par)
                    stack_k(n, group)
                sp.wait_ge(y_added, 1 + YADDS * (group + 1))
                sp.dma_start(out_v[bass.ds(group, 1)].rearrange("o p t d -> (o p) t d"), res[par][:])\
                  .then_inc(stored[par], 16)

            over_groups(sp, step)
            for s in stored:
                sp.wait_ge(s, 16 + 16 * GROUPS // 2)

        @block.gpsimd
        def _(pool):
            nc.gpsimd.memset(ident[:], 0.0).then_inc(c_ident, 1)
            pool.wait_ge(c_ident, 1)
            nc.gpsimd.affine_select(out=ident[:], in_=ident[:], compare_op=ALU.not_equal, fill=1.0, base=0,
                                    pattern=[[-1, P]], channel_multiplier=1).then_inc(c_ident, 1)
            nc.gpsimd.memset(minushalf[:], -0.5).then_inc(c_small, 1)
            nc.gpsimd.iota(iota8[:], pattern=[[1, E]], base=0, channel_multiplier=0,
                           allow_small_or_imprecise_dtypes=True).then_inc(c_small, 1)
            pool.wait_ge(c_small, 2)

            def xres_of(n, par, count):
                pool.wait_ge(x_in[par], count)
                nc.gpsimd.tensor_tensor(xres[par][:], xin[par][:],
                                        bo_b[:].unsqueeze(1).broadcast_to([P, NT, D]), ALU.add).then_inc(xres_done, 1)

            def inverse_deviation(n):
                pool.wait_ge(var_done, n + 1)
                nc.gpsimd.tensor_tensor(rstd[:], vareps[:], minushalf[:], ALU.pow).then_inc(rstd_done, 1)

            def mask_scores(n, k):
                pool.wait_ge(sc_copied, NG * UNITS * n + k + 1)
                pool.sem_inc(waited)
                if k % 3 == 0:
                    diag = sc[:, k % RING].rearrange("p (j k) -> p j k", j=NJ)
                else:
                    diag = sc[:, k % RING].rearrange("p (j k) -> p j k", j=2)[:, :, P:2 * P]
                nc.gpsimd.affine_select(out=diag, in_=diag, compare_op=ALU.is_ge, fill=MASKED, base=0,
                                        pattern=[[0, 2 if k % 3 else NJ], [-1, P]],
                                        channel_multiplier=1).then_inc(sc_masked, 1)

            def mask(group, p):
                pool.wait_ge(exp_done, PAIRS * group + p + 1)
                pool.sem_inc(waited)
                diag = pt[:, p % SLOTS, :, 0:2 * P]
                nc.gpsimd.affine_select(out=diag, in_=diag, compare_op=ALU.is_ge, fill=0.0, base=0,
                                        pattern=[[0, 2], [0, 2], [1, P]], channel_multiplier=-1).then_inc(p_masked, 1)

            def step(n, group, par):
                count = x_count(n, 1 - par)
                if group is None:
                    inverse_deviation(n)
                    nc.gpsimd.memset(kbd[0:ONE].bitcast(F32), 0.0).then_inc(c_kzero, 1)
                    pool.wait_ge(d_bias, 16 * (2 * NJ + 2))
                    xres_of(n, 1 - par, count)
                    for k in range(NG * UNITS):
                        mask_scores(n, k)
                    inverse_deviation(n + 1)
                    return
                for p in range(PAIRS):
                    mask(group, p)
                if n is not None:
                    xres_of(n, 1 - par, count)
                    if has_next(n):
                        inverse_deviation(n + 1)
                    for k in range(NG * UNITS):
                        mask_scores(n, k)

            over_groups(pool, step)

        @block.scalar
        def _(act):
            def split_x(n, par):
                act.wait_ge(xT_copied, n + 1)
                nc.scalar.activation(xThi[par][:], bank(("xT", 0))[:], ACT.Copy).then_inc(xT_hi, 1)

            def exp_pair(group, p):
                act.wait_ge(kq_scores, PAIRS * group + p + 1)
                nc.scalar.activation(pt[:, p % SLOTS], A[p % 2][:, :, 0:3 * P], ACT.Exp, scale=SCALE)\
                  .then_inc(exp_done, 1)

            def rows_of_max(n, par, g):
                act.wait_ge(mT_full, NG * n + g + 1)
                nc.scalar.activation(qst[par][ONE:ONE + ROWS_M, g, :], bank(("mT", g))[0:ROWS_M, :],
                                     ACT.Copy).then_inc(m_rows, 1)

            def hi_of_qk(n, o):
                act.wait_ge(qk_full, 2 * n + o + 1)
                if o == 0 and not (isinstance(n, int) and n == 0):
                    act.wait_ge(qk_stacked, STACKS * n)
                nc.scalar.activation(qkhi[o][:], bank(("qk", o))[:], ACT.Identity,
                                     bias=bqk[:, o:o + 1]).then_inc(qk_hi, 1)

            def copy_scores(n, par, slot):
                g, r = divmod(slot, SLOTS_G)
                if g > 0 and r == ROWS_AT:
                    rows_of_max(n, par, g - 1)
                if g < NG:
                    for k in range(PER_SLOT * slot, PER_SLOT * (slot + 1)):
                        act.wait_ge(qk_scores, NG * UNITS * n + k + 1)
                        if k >= RING:
                            act.wait_ge(max_done, NG * UNITS * n + k + 1 - RING)
                        nc.scalar.activation(sc[:, k % RING], bank(("scores", k))[:], ACT.Copy).then_inc(sc_copied, 1)

            def step(n, group, par):
                if group is None:
                    act.wait_ge(c_onecol, 1)

                    def ones_of_k(j):
                        nc.scalar.activation(kbd[ONE:ONE + ROWS_M, j].rearrange("p g t -> p (g t)"),
                                             onecol[ONE:ONE + ROWS_M, j:j + 1].broadcast_to([ROWS_M, NG * T]),
                                             ACT.Copy).then_inc(c_kzero, 1)

                    ones_of_k(0)
                    ones_of_k(1)
                    act.wait_ge(wT_copied, 2)
                    nc.scalar.activation(wqkhi[:], wqk[:], ACT.Copy).then_inc(wqk_hi, 1)
                    split_x(n, 1 - par)
                    ones_of_k(2)
                    act.wait_ge(d_bias, 16 * (2 * NJ + 2))
                    hi_of_qk(n, 0)
                    hi_of_qk(n, 1)
                    ones_of_k(3)
                    for hi, raw, there in ((w1hi, w1raw, d_w1), (w3hi, w3raw, d_w3)):
                        act.wait_ge(there, 32)
                        nc.scalar.activation(hi[:], raw, ACT.Copy).then_inc(wexp_hi, 1)
                    for slot in range(MAX_SLOTS):
                        copy_scores(n, 1 - par, slot)
                    for p in range(EARLY):
                        exp_pair(n, p)
                    return
                for p in range(EARLY, PAIRS):
                    exp_pair(group, p)
                    if p == EARLY + 1:
                        act.wait_ge(routed, ROUTE * group + 2 * NT + 2)
                        nc.scalar.activation(expgap[:], gap[:], ACT.Exp).then_inc(gap_exp, 1)
                    if p == X_AT and n is not None:
                        split_x(n, 1 - par)
                    if p in (QK_AT + 1, QK_AT + 3) and n is not None:
                        hi_of_qk(n, (p - QK_AT) // 2)
                for s in range(STEPS):
                    act.wait_ge(h1_full, STEPS * group + s + 1)
                    nc.scalar.activation(act1[s % 2][:], A[s % 2][:, 0, :], ACT.Silu).then_inc(silu_done, 1)
                    if s == 3:
                        act.wait_ge(onT_full, group + 1)
                        nc.scalar.activation(onT[:], bank(("onT", 0))[:], ACT.Copy).then_inc(onT_copied, 1)
                    if n is not None and s >= FIRST:
                        copy_scores(n, 1 - par, s - FIRST)
                if n is not None:
                    copy_scores(n, 1 - par, MAX_SLOTS - 1)
                    for p in range(EARLY):
                        exp_pair(n, p)

            over_groups(act, step)

        @block.vector
        def _(dve):
            dve.sem_inc(hid_done)
            dve.sem_inc(y_added)

            def attention_weights():
                dve.wait_ge(wT_ready, 1)
                for o in range(2):
                    nc.vector.tensor_copy(wqk[:, o, :].rearrange("p (j d g) -> p j g d", j=NJ, d=HD),
                                          A[0][:, 0, o * P:(o + 1) * P].rearrange("p (j g d) -> p j g d", j=NJ, d=HD))\
                      .then_inc(wT_copied, 1)
                nc.vector.tensor_copy(wvr[:, 0:P], A[0][:, 0, 2 * P:3 * P]).then_inc(wT_copied, 1)
                nc.vector.tensor_copy(woT[:], A[0][:, 0, 3 * P:4 * P]).then_inc(wT_copied, 1)

            def attention_weights_lo():
                dve.wait_ge(wqk_hi, 1)
                nc.vector.tensor_tensor(wqklo[:], wqk[:], wqkhi[:].bitcast(F32), ALU.subtract).then_inc(wqk_split, 1)

            def value_padding(i):
                nc.vector.memset(va[i][:], 0.0).then_inc(c_va, 1)
                dve.wait_ge(c_va, 2 * i + 1)
                nc.vector.memset(va[i][:, :, :, HD:HD + 1], 1.0).then_inc(c_va, 1)

            def copy_o(group, g):
                dve.wait_ge(o_full, NG * group + g + 1)
                nc.vector.tensor_copy(oT[:, g, :], Y[g % 2][:]).then_inc(o_copied, 1)

            def one_columns():
                dve.wait_ge(c_ident, 2)
                nc.vector.tensor_reduce(onecol[:], ident[:, ONE:ONE + ROWS_M].rearrange("p (j r) -> p j r", r=2),
                                        AX.X, ALU.add).then_inc(c_onecol, 1)

            def norm_stats(n, par, count):
                dve.wait_ge(x_in[par], count)
                for t in range(NT):
                    nc.vector.bn_stats(stats[:, t, :], xin[par][:, t, :]).then_inc(stats_done, 1)
                dve.wait_ge(stats_done, NT * (n + 1))
                dve.sem_inc(waited)
                for t in range(NT):
                    nc.vector.bn_aggr(mv[:, t, :], stats[:, t, :]).then_inc(mv_done, 1)
                dve.wait_ge(mv_done, NT * (n + 1))
                nc.vector.tensor_scalar(vareps[:], mv[:, :, 1], EPS, None, ALU.add).then_inc(var_done, 1)

            def norm_apply(n, par):
                dve.wait_ge(rstd_done, n + 1)
                for t in range(NT):
                    nc.vector.tensor_scalar(xn[:, t, :], xin[par][:, t, :], mv[:, t, 0:1], rstd[:, t:t + 1],
                                            ALU.subtract, ALU.mult).then_inc(xn_done, 1)

            def copy_x(n, par):
                dve.wait_ge(xT_full, n + 1)
                nc.vector.tensor_copy(xT[par][:], bank(("xT", 0))[:]).then_inc(xT_copied, 1)

            def lo_of_x(n, par):
                dve.wait_ge(xT_hi, n + 1)
                nc.vector.tensor_tensor(xTlo[par][:], xT[par][:], xThi[par][:].bitcast(F32),
                                        ALU.subtract).then_inc(xT_split, 1)

            def lo_of_qk(n, o):
                dve.wait_ge(qk_hi, 2 * n + o + 1)
                nc.vector.scalar_tensor_tensor(out=qklo[o][:], in0=bank(("qk", o))[:], scalar=bqk[:, o:o + 1],
                                               in1=qkhi[o][:].bitcast(F32), op0=ALU.add, op1=ALU.subtract)\
                  .then_inc(qk_split, 1)

            def copy_v(n, par, k):
                dve.wait_ge(vr_full, 2 * n + k + 1)
                src = bank(("vr", k))[:, 0:2 * (P + E)].rearrange("p (t c) -> p t c", t=2)
                for t in range(2):
                    last = nc.vector.tensor_tensor(va[par][:, 2 * k + t, :, 0:HD],
                                                   src[:, t, 0:P].rearrange("p (h d) -> p h d", d=HD),
                                                   bv_b[:].rearrange("p (h d) -> p h d", d=HD), ALU.add)
                last.then_inc(v_copied, 1)
                nc.vector.tensor_copy(lg[par][:, 2 * k:2 * k + 2, :], src[:, :, P:P + E]).then_inc(lg_copied, 1)

            def route_top(group, par):
                dve.wait_ge(lg_copied, 2 * (group + 1))
                dve.sem_inc(waited)
                for t in range(NT):
                    nc.vector.max(top[:, t, :], lg[par][:, t, :]).then_inc(routed, 1)
                dve.wait_ge(routed, ROUTE * group + NT)
                dve.sem_inc(waited)
                for t in range(NT):
                    nc.vector.max_index(topi[:, t, :], top[:, t, :], lg[par][:, t, :]).then_inc(routed, 1)
                dve.wait_ge(routed, ROUTE * group + 2 * NT)
                nc.vector.tensor_copy(topf[:], topi[:]).then_inc(routed, 1)
                nc.vector.tensor_tensor(gap[:], top[:, :, 1], top[:, :, 0], ALU.subtract).then_inc(routed, 1)

            def route_gates(group):
                k = ROUTE * group + 2 * NT + 2
                dve.wait_ge(routed, k)
                for hot, which in ((hot1, 0), (hot2, 1)):
                    nc.vector.tensor_tensor(hot[:], iota8[:].unsqueeze(1).broadcast_to([P, NT, E]),
                                            topf[:, :, which:which + 1].broadcast_to([P, NT, E]),
                                            ALU.is_equal).then_inc(routed, 1)
                dve.wait_ge(gap_exp, group + 1)
                nc.vector.tensor_scalar(gden[:], expgap[:], 1.0, None, ALU.add).then_inc(routed, 1)
                dve.wait_ge(routed, k + 3)
                nc.vector.reciprocal(gate1[:], gden[:]).then_inc(routed, 1)
                dve.wait_ge(routed, k + 4)
                nc.vector.tensor_tensor(cw1[:], hot1[:], gate1[:].unsqueeze(2).broadcast_to([P, NT, E]),
                                        ALU.mult)
                nc.vector.tensor_tensor(gate2[:], expgap[:], gate1[:], ALU.mult).then_inc(routed, 1)
                dve.wait_ge(routed, k + 5)
                nc.vector.tensor_tensor(cw2[:], hot2[:], gate2[:].unsqueeze(2).broadcast_to([P, NT, E]),
                                        ALU.mult).then_inc(routed, 1)
                dve.wait_ge(routed, k + 6)
                nc.vector.tensor_tensor(cw[:], cw1[:], cw2[:], ALU.add).then_inc(routed, 1)

            def row_maxima(n, k):
                b, u = divmod(k % UNITS, 3)
                g = k // UNITS
                src = sc[:, k % RING]
                dve.wait_ge(sc_masked, UNITS * NG * n + k + 1)
                if u == 0:
                    o, i = mx[:, g, QT * b, :], src.rearrange("p (j k) -> p j k", j=NJ)
                else:
                    o, i = mx[:, g, QT * b + 1, 2 * u - 2:2 * u], src.rearrange("p (j k) -> p j k", j=2)
                nc.vector.reduce_max(o, i, AX.X).then_inc(max_done, 1)

            def split_max(n, g):
                hi, lo = mcol[:, g % 2, :, :, 0], mcol[:, g % 2, :, :, 1]
                dve.wait_ge(max_done, UNITS * (NG * n + g + 1))
                nc.vector.tensor_scalar(hi.bitcast(F32R), mx[:, g], -1.0, None, ALU.mult).then_inc(m_split, 1)
                dve.wait_ge(m_split, 2 * (NG * n + g) + 1)
                nc.vector.scalar_tensor_tensor(out=lo.bitcast(F32R), in0=mx[:, g], scalar=-1.0, in1=hi, op0=ALU.mult,
                                               op1=ALU.subtract).then_inc(m_split, 1)

            def maxima(n, slot):
                g, k = divmod(slot, SLOTS_G)
                if g < NG:
                    for u in range(PER_SLOT):
                        row_maxima(n, PER_SLOT * slot + u)
                    if k == SLOTS_G - 1:
                        split_max(n, g)

            def normalise(group, t):
                src = bank(("oN", t))[:].rearrange("p (g j r) -> p g j r", g=NG, r=ROWS)
                dve.wait_ge(oN_full, NT * group + t + 1)
                r = rec[:, t, :].rearrange("p (g j) -> p g j", j=NJ)
                nc.vector.reciprocal(r, src[:, :, :, HD]).then_inc(rec_done, 1)
                dve.wait_ge(rec_done, NT * group + t + 1)
                nc.vector.tensor_tensor(on[:, t, :].rearrange("p (j g d) -> p g j d", g=NG, d=HD), src[:, :, :, 0:HD],
                                        r.unsqueeze(3).broadcast_to([P, NG, NJ, HD]), ALU.mult).then_inc(on_done, 1)

            def hidden(group, s):
                dve.wait_ge(h3_full, STEPS * group + s + 1)
                dve.wait_ge(silu_done, STEPS * group + s + 1)
                nc.vector.tensor_tensor(hid[s // NH % 2][:, s % NH, :], act1[s % 2][:], A[s % 2][:, 1, :],
                                        ALU.mult).then_inc(hid_done, 1)

            def add_expert(group, par, e):
                dve.wait_ge(y_full, NE * group + e + 1)
                if e == 0:
                    dve.wait_ge(xres_done, group + 1)
                if e < E:
                    for t in range(NT):
                        if e > 0:
                            dve.wait_ge(y_added, 1 + YADDS * group + NT * (e - 1) + t + 1)
                        before = xres[par] if e == 0 else acc
                        nc.vector.scalar_tensor_tensor(out=acc[:, t, :], in0=Y[e % 2][:, t * D:(t + 1) * D],
                                                       scalar=cw[:, t, e:e + 1], in1=before[:, t, :],
                                                       op0=ALU.mult, op1=ALU.add).then_inc(y_added, 1)
                else:
                    dve.wait_ge(y_added, 1 + YADDS * group + NT * E)
                    dve.wait_ge(stored[par], 16 + 8 * group - (8 if par else 0))
                    nc.vector.tensor_tensor(res[par][:], acc[:], Y[e % 2][:].rearrange("p (t d) -> p t d", d=D),
                                            ALU.add).then_inc(y_added, 1)

            def step(n, group, par):
                count = x_count(n, 1 - par)
                if group is None:
                    one_columns()
                    value_padding(0)
                    norm_stats(n, 1 - par, count)
                    attention_weights()
                    norm_apply(n, 1 - par)
                if n is not None:
                    copy_x(n, 1 - par)
                if group is None:
                    attention_weights_lo()
                else:
                    route_top(group, par)
                    route_gates(group)
                if n is not None:
                    lo_of_x(n, 1 - par)
                    if group is None:
                        dve.wait_ge(d_bias, 16 * (2 * NJ + 2))
                    copy_v(n, 1 - par, 0)
                    copy_v(n, 1 - par, 1)
                if group is not None:
                    copy_o(group, 0)
                if n is not None:
                    lo_of_qk(n, 0)
                    lo_of_qk(n, 1)
                if group is None:
                    value_padding(1)
                else:
                    copy_o(group, 1)
                    copy_o(group, 2)
                if group is None:
                    for k, (lo, raw, hi) in enumerate(((w1lo, w1raw, w1hi), (w3lo, w3raw, w3hi))):
                        dve.wait_ge(wexp_hi, k + 1)
                        nc.vector.tensor_tensor(lo[:], raw, hi[:].bitcast(F32), ALU.subtract).then_inc(wexp_split, 1)
                    for slot in range(MAX_SLOTS):
                        if slot > 0:
                            maxima(n, slot - 1)
                    norm_stats(n + 1, par, 16)
                    norm_apply(n + 1, par)
                    return
                for e in range(NE):
                    for hh in range(NH):
                        s = NH * e + hh
                        hidden(group, s)
                        if s == 0:
                            copy_o(group, NG - 1)
                        if has_next(n):
                            if s == 3:
                                norm_stats(n + 1, par, x_count(n + 1, par))
                            if s == 4:
                                norm_apply(n + 1, par)
                        if s in (1, 2):
                            normalise(group, 2 * s - 2)
                            normalise(group, 2 * s - 1)
                        if n is not None and s > FIRST:
                            maxima(n, s - FIRST - 1)
                    if e > 0:
                        add_expert(group, par, e - 1)
                add_expert(group, par, NE - 1)

            over_groups(dve, step)

        @block.tensor
        def _(pe):
            pe.wait_ge(c_ident, 2)
            pe.wait_ge(d_watt, 16 * 5)
            for k in range(4):
                last = nc.tensor.transpose(A[0][:, 0, k * P:(k + 1) * P], wraw[:, k, :], ident[:])
            last.then_inc(wT_ready, 1)

            def three(o, hi, lo, xhi, xlo):
                nc.tensor.matmul(o, hi, xhi, start=True, stop=False)
                nc.tensor.matmul(o, hi, xlo, start=False, stop=False)
                return nc.tensor.matmul(o, lo, xhi, start=False, stop=True)

            def transpose_x(n, group):
                bank_free(pe, ("xT", 0), n, group)
                pe.wait_ge(xn_done, NT * (n + 1))
                for t in range(NT):
                    last = nc.tensor.transpose(bank(("xT", 0))[:, t * P:(t + 1) * P], xn[:, t, :], ident[:])
                last.then_inc(xT_full, 1)

            def project_qk(n, group, par):
                pe.wait_ge(xT_split, n + 1)
                for o in range(2):
                    bank_free(pe, ("qk", o), n, group)
                    three(bank(("qk", o))[:], wqkhi[:, o, :], wqklo[:, o, :], xThi[par][:], xTlo[par][:])\
                        .then_inc(qk_full, 1)

            def project_v(n, group, par):
                pe.wait_ge(xT_copied, n + 1)
                for k in range(2):
                    bank_free(pe, ("vr", k), n, group)
                    for t in range(2):
                        last = nc.tensor.matmul(bank(("vr", k))[:, t * (P + E):(t + 1) * (P + E)],
                                                xT[par][:, (2 * k + t) * P:(2 * k + t + 1) * P], wvr[:],
                                                start=True, stop=True)
                    last.then_inc(vr_full, 1)

            def scores(n, group, par, k):
                g = k // UNITS
                b, u = divmod(k % UNITS, 3)
                if k == 0:
                    pe.wait_ge(qk_stacked, STACKS * (n + 1))
                o = bank(("scores", k))
                bank_free(pe, ("scores", k), n, group)
                at = b * S + (P if u else 0)
                q, keys = qst[par][0:ONE, g, at:at + P], kbd[0:ONE, :, g]
                if u == 0:
                    last = nc.tensor.matmul(o[:].rearrange("p (j k) -> p j k", j=NJ), q, keys[:, :, at:at + P],
                                            start=True, stop=True)
                else:
                    last = nc.tensor.matmul(o[:].rearrange("p (j k) -> p j k", j=2), q,
                                            keys[:, 2 * u - 2:2 * u, b * S:(b + 1) * S], start=True, stop=True)
                last.then_inc(qk_scores, 1)

            def transpose_max(n, group, g):
                bank_free(pe, ("mT", g), n, group)
                pe.wait_ge(m_split, 2 * (NG * n + g + 1))
                for t in range(NT):
                    last = nc.tensor.transpose(bank(("mT", g))[0:ROWS_M, t * P:(t + 1) * P],
                                               mcol[:, g % 2, t].rearrange("p j r -> p (j r)"), ident[:])
                last.then_inc(mT_full, 1)

            def prepare_maxima(n, group, par, slot):
                if slot < NG * SLOTS_G:
                    for k in range(PER_SLOT * slot, PER_SLOT * (slot + 1)):
                        scores(n, group, par, k)

            def prepare_rows(n, group, slot):
                g, k = divmod(slot, SLOTS_G)
                if g > 0 and k == ROWS_AT:
                    transpose_max(n, group, g - 1)

            def of_pair(p):
                g, r = divmod(p, SEQS * 2)
                return g, r // 2, (r % 2) * 2

            def pair_scores(group, par, p):
                g, b, j0 = of_pair(p)
                if p < 2 and not (isinstance(group, int) and group == 0):
                    pe.wait_ge(hid_done, STEPS * group + p)
                if p % 4 == 0:
                    pe.wait_ge(m_rows, NG * group + g + 1)
                if p >= 2:
                    pe.wait_ge(exp_done, PAIRS * group + p - 1)
                keys = kbd[0:ONE + ROWS_M, :, g]
                for a in range(2):
                    o = A[p % 2][:, a, 0:3 * P].rearrange("p (c q) -> p c q", q=P)
                    for kt, columns in ((1, o[:, 0:2]), (0, o[:, 0:3:2])):
                        last = nc.tensor.matmul(columns, keys[:, j0 + a, b * S + kt * P:b * S + (kt + 1) * P],
                                                qst[par][0:ONE + ROWS_M, g, b * S:(b + 1) * S].rearrange("p (c q) -> p c q", q=P),
                                                start=True, stop=True)
                last.then_inc(kq_scores, 1)

            def pair_output(group, par, p):
                g, b, j0 = of_pair(p)
                if p == 0:
                    pe.wait_ge(v_copied, 2 * (group + 1))
                    pe.wait_ge(y_added, 1 + YADDS * group)
                if p % 4 == 0 and g >= 2:
                    pe.wait_ge(o_copied, NG * group + g - 1)
                pe.wait_ge(p_masked, PAIRS * group + p + 1)
                for a in range(2):
                    j = j0 + a
                    o = Y[g % 2][ROWS * j:ROWS * (j + 1), b * S:(b + 1) * S]
                    h = NG * j + g
                    pr = pt[:, p % SLOTS, a, :].rearrange("p (c q) -> p c q", q=P)
                    nc.tensor.matmul(o.rearrange("p (c q) -> p c q", q=P), va[par][:, QT * b, h, :], pr[:, 0:3:2],
                                     start=True, stop=False)
                    last = nc.tensor.matmul(o[:, P:2 * P], va[par][:, QT * b + 1, h, :], pr[:, 1],
                                            start=False, stop=True)
                if p % 4 == 3:
                    last.then_inc(o_full, 1)

            def up(n, group, par, s):
                e, hh = divmod(s, NH)
                if s < 2:
                    pe.wait_ge(exp_done, PAIRS * (group + 1) - 1 + s)
                else:
                    pe.wait_ge(hid_done, STEPS * group + s)
                c = slice(hh * P, (hh + 1) * P)
                three(A[s % 2][:, 0, :], w1hi[:, e, c], w1lo[:, e, c], xThi[par][:], xTlo[par][:])\
                    .then_inc(h1_full, 1)
                if n is not None and s >= FIRST:
                    prepare_rows(n, group, s - FIRST)
                three(A[s % 2][:, 1, :], w3hi[:, e, c], w3lo[:, e, c], xThi[par][:], xTlo[par][:])\
                    .then_inc(h3_full, 1)

            def down(group, e):
                if e < 2:
                    pe.wait_ge(o_copied, NG * (group + 1) - 1 + e)
                else:
                    pe.wait_ge(y_added, 1 + YADDS * group + NT * (e - 1))
                pe.wait_ge(hid_done, 1 + STEPS * group + NH * (e + 1))
                if e == NE - 1:
                    pe.wait_ge(onT_copied, group + 1)
                for t in range(NT):
                    o, c = Y[e % 2][:, t * D:(t + 1) * D], slice(t * P, (t + 1) * P)
                    for hh in range(NH):
                        last = nc.tensor.matmul(o, hid[e % 2][:, hh, c], w2s[:, e, hh, :], start=(hh == 0),
                                                stop=(hh == NH - 1 and e < NE - 1))
                    if e == NE - 1:
                        last = nc.tensor.matmul(o, onT[:, c], woT[:], start=False, stop=True)
                last.then_inc(y_full, 1)

            def attention_rows(n, group, t):
                bank_free(pe, ("oN", t), n, group)
                if t == 0:
                    pe.wait_ge(o_copied, NG * (group + 1))
                for g in range(NG):
                    last = nc.tensor.transpose(bank(("oN", t))[:, g * P:(g + 1) * P], oT[:, g, t * P:(t + 1) * P],
                                               ident[:])
                last.then_inc(oN_full, 1)

            def attention_columns(n, group):
                bank_free(pe, ("onT", 0), n, group)
                pe.wait_ge(on_done, NT * (group + 1))
                for t in range(NT):
                    last = nc.tensor.transpose(bank(("onT", 0))[:, t * P:(t + 1) * P], on[:, t, :], ident[:])
                last.then_inc(onT_full, 1)

            def step(n, group, par):
                if group is None:
                    transpose_x(n, group)
                    pe.wait_ge(wT_copied, 4)
                    project_v(n, group, 1 - par)
                    pe.wait_ge(wqk_split, 1)
                    project_qk(n, group, 1 - par)
                    for slot in range(MAX_SLOTS):
                        prepare_rows(n, group, slot)
                        prepare_maxima(n, group, 1 - par, slot)
                    pe.wait_ge(wexp_split, 2)
                    pe.wait_ge(d_w2, 16 * NE)
                    pe.wait_ge(c_va, 4)
                    for p in range(EARLY):
                        pair_scores(n, 1 - par, p)
                    return
                lag = 3
                for p in range(EARLY, PAIRS + lag):
                    if p < PAIRS:
                        pair_scores(group, par, p)
                    if n is not None:
                        if p == X_AT:
                            transpose_x(n, group)
                        if p == V_AT:
                            project_v(n, group, 1 - par)
                        if p == QK_AT:
                            project_qk(n, group, 1 - par)
                    if p == PAIRS + lag - 2:
                        up(n, group, par, 0)
                    if p >= lag:
                        pair_output(group, par, p - lag)
                for e in range(NE):
                    for hh in range(NH):
                        s = NH * e + hh
                        if s > 0:
                            up(n, group, par, s)
                        if s in (1, 2):
                            attention_rows(n, group, 2 * s - 2)
                            attention_rows(n, group, 2 * s - 1)
                        if s == 3:
                            attention_columns(n, group)
                        if n is not None and s >= FIRST:
                            prepare_maxima(n, group, 1 - par, s - FIRST)
                    if e > 0:
                        down(group, e - 1)
                if n is not None:
                    prepare_rows(n, group, MAX_SLOTS - 1)
                    for p in range(EARLY):
                        pair_scores(n, 1 - par, p)
                down(group, NE - 1)

            over_groups(pe, step)


_INS = ["L0_attn_x", "L0_attn_Wq", "L0_attn_bq", "L0_attn_Wk", "L0_attn_bk", "L0_attn_Wv", "L0_attn_bv", "L0_attn_Wo",
        "L0_attn_bo", "L0_ffn_w_router", "L0_ffn_w1", "L0_ffn_w3", "L0_ffn_w2", "L0_ffn_sw1", "L0_ffn_sw3",
        "L0_ffn_sw2"]


def kernel(**inputs):
    import numpy as _np
    import concourse.bacc as _bacc
    from concourse.bass_utils import run_bass_kernel_spmd as _run

    nc = _bacc.Bacc("TRN2", target_bir_lowering=False, num_devices=1)
    arrays, args = {}, []
    for name in _INS:
        a = _np.ascontiguousarray(inputs[name])
        arrays[f"in_{name}"] = a
        args.append(nc.dram_tensor(f"in_{name}", a.shape, mybir.dt.from_np(a.dtype), kind="ExternalInput").ap())
    shape = arrays["in_L0_attn_x"].shape
    args.append(nc.dram_tensor("out_0", shape, F32, kind="ExternalOutput").ap())
    program(nc, *args)
    r = _run(nc, [arrays], core_ids=[0])
    return r.results[0]["out_0"]
```

```python
from contextlib import ExitStack

import concourse.bass as bass
from concourse import mybir

F32 = mybir.dt.float32
F32R = mybir.dt.float32r
U32 = mybir.dt.uint32
ALU = mybir.AluOpType
ACT = mybir.ActivationFunctionType
AX = mybir.AxisListType

P = 128
BANK = 512
NJ = 4
ROWS = P // NJ
HALF = ROWS // 2
EPS = 1e-5
MASKED = -3.0e38


def program(nc, x, wq, bq, wk, bk, wv, bv, wo, bo, w_router, w1, w3, w2, sw1, sw3, sw2, out):
    B, S, D = x.shape
    E, _, HID = w1.shape
    HD = 8
    H = D // HD
    NG = H // NJ
    NC = NG // 2
    SEQS = 2
    T = SEQS * S
    NT = T // P
    QT = S // P
    GROUPS = B // SEQS
    NE = E + 1
    NH = HID // P
    STEPS = NE * NH
    PAIRS = NG * SEQS * NJ // 2
    UNITS = SEQS * 3
    SLOTS = 4
    RING = 4
    CHUNKS = 3
    SCALE = float(HD) ** -0.5
    ONE = 3 * NJ * HD
    ROWS_M = 2 * NJ
    assert D == P and T == BANK and QT == 2 and NH == 2 and GROUPS % 2 == 0 and E == 8

    x_v = x.rearrange("(g s) (t p) d -> g p (s t) d", s=SEQS, p=P)
    out_v = out.rearrange("(g s) (t p) d -> g p (s t) d", s=SEQS, p=P)

    with ExitStack() as ctx:
        def sb(name, shape, dt=F32):
            return ctx.enter_context(nc.sbuf_tensor(name, shape, dt))

        def sem(name):
            return ctx.enter_context(nc.semaphore(name))

        w1hi, w1lo = sb("w1hi", [P, NE, HID], F32R), sb("w1lo", [P, NE, HID], F32R)
        w3hi, w3lo = sb("w3hi", [P, NE, HID], F32R), sb("w3lo", [P, NE, HID], F32R)
        w2s = sb("w2s", [P, NE, NH, D])
        wraw = sb("wraw", [P, 4, P])
        wqk = sb("wqk", [P, 2, P])
        wqkhi, wqklo = sb("wqkhi", [P, 2, P], F32R), sb("wqklo", [P, 2, P], F32R)
        wvr = sb("wvr", [P, P + E])
        woT = sb("woT", [P, P])
        braw, bqk = sb("braw", [P, 2]), sb("bqk", [P, 2])
        order = sb("order", [P, P])
        bv_b, bo_b = sb("bv_b", [P, P]), sb("bo_b", [P, P])
        ident = sb("ident", [P, P])
        onecol = sb("onecol", [P, NJ])
        iota8 = sb("iota8", [P, E])
        minushalf = sb("minushalf", [P, NT])

        xin = [sb(f"xin{i}", [P, NT, D]) for i in range(2)]
        xres = [sb(f"xres{i}", [P, NT, D]) for i in range(2)]
        stats, mv = sb("stats", [P, NT, 6]), sb("mv", [P, NT, 2])
        vareps, rstd = sb("vareps", [P, NT]), sb("rstd", [P, NT])
        xn = sb("xn", [P, NT, D])
        xT = [sb(f"xT{i}", [P, T]) for i in range(2)]
        xThi = [sb(f"xThi{i}", [P, T], F32R) for i in range(2)]
        xTlo = [sb(f"xTlo{i}", [P, T], F32R) for i in range(2)]
        qkhi = [sb(f"qkhi{i}", [P, T], F32R) for i in range(2)]
        qklo = [sb(f"qklo{i}", [P, T], F32R) for i in range(2)]
        qst = [sb(f"qst{i}", [P, NG, T], F32R) for i in range(2)]
        kbd = sb("kbd", [P, NJ, NG, T], F32R)
        va = [sb(f"va{i}", [P, NT, H // 2, 3, HALF]) for i in range(2)]
        sc = sb("sc", [P, RING, BANK])
        mx = sb("mx", [P, NG, NT, NJ])
        mcol = sb("mcol", [P, NC, NT, 2, P // 2])
        pt = sb("pt", [P, SLOTS, 2, 3 * P])
        oT = sb("oT", [P, NC, T])
        rec, on = sb("rec", [P, NT, H]), sb("on", [P, NT, D])
        onT = sb("onT", [P, T])
        lg = [sb(f"lg{i}", [P, NT, E]) for i in range(2)]
        top, topi, topf = sb("top", [P, NT, 8]), sb("topi", [P, NT, 8], U32), sb("topf", [P, NT, 8])
        gap, expgap, gden = sb("gap", [P, NT]), sb("expgap", [P, NT]), sb("gden", [P, NT])
        gate1, gate2 = sb("gate1", [P, NT]), sb("gate2", [P, NT])
        hot1, hot2 = sb("hot1", [P, NT, E]), sb("hot2", [P, NT, E])
        cw1, cw2, cw = sb("cw1", [P, NT, E]), sb("cw2", [P, NT, E]), sb("cw", [P, NT, E])
        act1 = [sb(f"act1_{i}", [P, T]) for i in range(2)]
        hid = [sb(f"hid{i}", [P, NH, T]) for i in range(2)]
        res = [sb(f"res{i}", [P, NT, D]) for i in range(2)]

        w1raw = pt[:].rearrange("p s a c -> p (s a c)")[:, 0:NE * HID].rearrange("p (e h) -> p e h", h=HID)
        w3raw = sb("w3raw", [P, NE, HID])

        A = [ctx.enter_context(nc.psum_tensor(f"A{i}", [P, 2, BANK], F32)) for i in range(2)]
        Y = [ctx.enter_context(nc.psum_tensor(f"Y{i}", [P, BANK], F32)) for i in range(2)]
        M = [ctx.enter_context(nc.psum_tensor(f"M{i}", [P, BANK], F32)) for i in range(2)]

        d_watt, d_w2, d_bias = sem("d_watt"), sem("d_w2"), sem("d_bias")
        d_w1, d_w3 = [sem(f"d_w1_{k}") for k in range(CHUNKS)], [sem(f"d_w3_{k}") for k in range(CHUNKS)]
        c_ident, c_small, c_kzero = sem("c_ident"), sem("c_small"), sem("c_kzero")
        c_va, c_onecol, c_mcol = [sem(f"c_va{i}") for i in range(2)], sem("c_onecol"), sem("c_mcol")
        wT_ready, wT_copied = sem("wT_ready"), sem("wT_copied")
        bias_full, bias_ready = sem("bias_full"), sem("bias_ready")
        wqk_hi, wqk_split = sem("wqk_hi"), sem("wqk_split")
        wexp_hi = sem("wexp_hi")
        wexp_split = [sem(f"wexp_split{k}") for k in range(CHUNKS)]
        waited = sem("waited")
        x_in = [sem(f"x_in{i}") for i in range(2)]
        stored = [sem(f"stored{i}") for i in range(2)]
        xres_done = sem("xres_done")
        stats_done = sem("stats_done")
        mv_done = sem("mv_done")
        var_done = sem("var_done")
        rstd_done = sem("rstd_done")
        xn_done = sem("xn_done")
        xT_full = sem("xT_full")
        xT_copied = sem("xT_copied")
        xT_hi = sem("xT_hi")
        xT_split = sem("xT_split")
        qk_full = sem("qk_full")
        qk_hi = sem("qk_hi")
        qk_split = sem("qk_split")
        qk_stacked = sem("qk_stacked")
        vr_full = sem("vr_full")
        v_copied = sem("v_copied")
        lg_copied = sem("lg_copied")
        routed = sem("routed")
        gap_exp = sem("gap_exp")
        qk_scores = sem("qk_scores")
        sc_copied = sem("sc_copied")
        sc_masked = sem("sc_masked")
        max_done = sem("max_done")
        m_split = sem("m_split")
        mT_full = sem("mT_full")
        m_rows = sem("m_rows")
        kq_scores = sem("kq_scores")
        exp_done = sem("exp_done")
        p_masked = sem("p_masked")
        o_full = sem("o_full")
        o_copied = sem("o_copied")
        oN_full = sem("oN_full")
        rec_done = sem("rec_done")
        on_done = sem("on_done")
        onT_full = sem("onT_full")
        onT_copied = sem("onT_copied")
        h1_full = sem("h1_full")
        h3_full = sem("h3_full")
        silu_done = sem("silu_done")
        hid_done = sem("hid_done")
        y_full = sem("y_full")
        attn_full = sem("attn_full")
        attn_added = sem("attn_added")
        y_added = sem("y_added")
        STACKS = 16 * (3 + 3 * NJ)
        ROUTE = 2 * NT + 9
        YADDS = E * NT + 1
        PER_SLOT = 2
        EARLY = 2
        X_AT, V_AT, QK_AT = 2, 4, 6
        GAP_AT = 9
        FIRST = 4
        SLOTS_G = UNITS // PER_SLOT
        ROWS_AT = 2
        MAX_SLOTS = NG * SLOTS_G + ROWS_AT + 1

        USES = [("xT", 0), ("vr", 0), ("vr", 1), ("qk", 0), ("qk", 1)]
        USES += [("oN", k) for k in range(NT // 2)] + [("onT", 0)]
        FINISH = set(USES[5:])
        for slot in range(MAX_SLOTS):
            g, k = divmod(slot, SLOTS_G)
            if g > 0 and g % 2 == 0 and k == ROWS_AT:
                USES += [("mT", g // 2 - 1)]
            if g < NG:
                USES += [("scores", PER_SLOT * slot + u) for u in range(PER_SLOT)]
        assert STEPS - FIRST == MAX_SLOTS - 1
        assert len(USES) % 2 == 0

        def bank(use):
            return M[USES.index(use) % 2]

        def freed(use, n, group):
            at = USES.index(use)
            before = [k for k in range(at % 2, at, 2) if (group if USES[k] in FINISH else n) is not None]
            if before:
                kind, k = USES[before[-1]]
                base = n if (kind, k) not in FINISH else group
            elif group is None:
                return None
            else:
                kind, k = USES[len(USES) - 2 + at % 2]
                base = group
            done, each = {"xT": (xT_copied, 1), "qk": (qk_split, 2), "vr": (lg_copied, 2), "oN": (on_done, NT // 2),
                          "onT": (onT_copied, 1), "scores": (sc_copied, NG * UNITS), "mT": (m_rows, NG)}[kind]
            return done, base * each + (k + 1) * (2 if kind == "mT" else 1)

        def bank_free(pe, use, n, group):
            wait = freed(use, n, group)
            if wait:
                pe.wait_ge(*wait)

        def over_groups(eng, step):
            step(0, None, 1)
            with eng.Fori(0, GROUPS // 2 - 1) as i:
                step(i * 2 + 1, i * 2, 0)
                step(i * 2 + 2, i * 2 + 1, 1)
            step(GROUPS - 1, GROUPS - 2, 0)
            step(None, GROUPS - 1, 1)

        def chunk(k):
            return slice(k * NE // CHUNKS, (k + 1) * NE // CHUNKS)

        def has_next(n):
            return n is not None and not (isinstance(n, int) and n == GROUPS - 1)

        def x_count(n, par):
            return None if n is None else 8 * n + (8 if par else 16)

        def split_experts(eng, k, i):
            at, (lo, raw, hi) = chunk(k), ((w1lo, w1raw, w1hi), (w3lo, w3raw, w3hi))[i]
            eng.wait_ge(wexp_hi, 2 * k + i + 1)
            eng.tensor_tensor(lo[:, at], raw[:, at], hi[:, at].bitcast(F32), ALU.subtract).then_inc(wexp_split[k], 1)

        def value_padding(eng, i):
            eng.memset(va[i][:], 0.0).then_inc(c_va[i], 1)
            eng.wait_ge(c_va[i], 1)
            eng.memset(va[i][:, :, :, 0:3:2, HD:HD + 1], 1.0).then_inc(c_va[i], 1)

        block = ctx.enter_context(nc.Block())

        @block.sync
        def _(sp):
            for s in stored:
                sp.sem_inc(s, 16)
            sp.dma_start(xin[0][:], x_v[0]).then_inc(x_in[0], 16)
            for n, w in enumerate((wq, wk, wv, wo)):
                sp.dma_start(wraw[:, n, :], w).then_inc(d_watt, 16)
            sp.dma_start(wvr[:, P:P + E], w_router).then_inc(d_watt, 16)
            for o, b in enumerate((bq, bk)):
                sp.dma_start(braw[:, o:o + 1], b.rearrange("(p o) -> p o", o=1),
                             allow_slow_non_contiguous=True).then_inc(d_bias, 16)
            for b, t in ((bv, bv_b), (bo, bo_b)):
                sp.dma_start(t[:], b.partition_broadcast(P)).then_inc(d_bias, 16)
            for k in range(CHUNKS):
                first, last = chunk(k).start, chunk(k).stop
                for raw, w, sw, there in ((w1raw, w1, sw1, d_w1[k]), (w3raw, w3, sw3, d_w3[k])):
                    sp.dma_start(raw[:, first:min(last, E), :],
                                 w[first:min(last, E)].rearrange("e d h -> d e h")).then_inc(there, 16)
                    if last == NE:
                        sp.dma_start(raw[:, E, :], sw).then_inc(there, 16)
            for e in range(E):
                sp.dma_start(w2s[:, e], w2[e].rearrange("(a p) d -> p a d", p=P)).then_inc(d_w2, 16)
            sp.dma_start(w2s[:, E], sw2.rearrange("(a p) d -> p a d", p=P)).then_inc(d_w2, 16)
            sp.dma_start(xin[1][:], x_v[1]).then_inc(x_in[1], 16)

            def stack_q(n, par):
                sp.wait_ge(qk_split, 2 * n + 1)
                for r, part in enumerate((qkhi[0], qkhi[0], qklo[0])):
                    sp.dma_start(qst[par][NJ * HD * r:NJ * HD * (r + 1)].bitcast(F32), part[:].bitcast(F32))\
                      .then_inc(qk_stacked, 16)

            def stack_k(n, group):
                sp.wait_ge(qk_split, 2 * n + 2)
                sp.sem_inc(waited)
                if group is None:
                    sp.wait_ge(c_kzero, 1 + NJ)
                else:
                    sp.wait_ge(kq_scores, PAIRS * (group + 1))
                for r, part in enumerate((qkhi[1], qklo[1], qkhi[1])):
                    for j in range(NJ):
                        at = HD * (NJ * r + j)
                        sp.dma_start(kbd[at:at + HD, j].bitcast(F32), part[ROWS * j:ROWS * (j + 1), :].bitcast(F32))\
                          .then_inc(qk_stacked, 16)

            def step(n, group, par):
                if group is None:
                    stack_q(n, 1 - par)
                    stack_k(n, group)
                    return
                if has_next(n):
                    sp.wait_ge(xn_done, NT * (group + 1))
                    sp.wait_ge(xres_done, group + 1)
                    sp.dma_start(xin[par][:], x_v[bass.ds(n + 1, 1)].rearrange("o p t d -> (o p) t d"))\
                      .then_inc(x_in[par], 16)
                if n is not None:
                    stack_q(n, 1 - par)
                    stack_k(n, group)
                sp.wait_ge(attn_added, group + 1)
                sp.dma_start(out_v[bass.ds(group, 1)].rearrange("o p t d -> (o p) t d"), res[par][:])\
                  .then_inc(stored[par], 16)

            over_groups(sp, step)
            for s in stored:
                sp.wait_ge(s, 16 + 16 * GROUPS // 2)

        @block.gpsimd
        def _(pool):
            nc.gpsimd.memset(ident[:], 0.0).then_inc(c_ident, 1)
            pool.wait_ge(c_ident, 1)
            nc.gpsimd.affine_select(out=ident[:], in_=ident[:], compare_op=ALU.not_equal, fill=1.0, base=0,
                                    pattern=[[-1, P]], channel_multiplier=1).then_inc(c_ident, 1)
            nc.gpsimd.memset(minushalf[:], -0.5).then_inc(c_small, 1)
            nc.gpsimd.iota(iota8[:], pattern=[[1, E]], base=0, channel_multiplier=0,
                           allow_small_or_imprecise_dtypes=True).then_inc(c_small, 1)
            pool.wait_ge(c_small, 2)

            def xres_of(n, par, count):
                pool.wait_ge(x_in[par], count)
                nc.gpsimd.tensor_tensor(xres[par][:], xin[par][:],
                                        bo_b[:].unsqueeze(1).broadcast_to([P, NT, D]), ALU.add).then_inc(xres_done, 1)

            def inverse_deviation(n):
                pool.wait_ge(var_done, n + 1)
                nc.gpsimd.tensor_tensor(rstd[:], vareps[:], minushalf[:], ALU.pow).then_inc(rstd_done, 1)

            def mask_scores(n, k):
                pool.wait_ge(sc_copied, NG * UNITS * n + k + 1)
                pool.sem_inc(waited)
                if k % 3 == 0:
                    diag = sc[:, k % RING].rearrange("p (j k) -> p j k", j=NJ)
                else:
                    diag = sc[:, k % RING].rearrange("p (j k) -> p j k", j=2)[:, :, P:2 * P]
                nc.gpsimd.affine_select(out=diag, in_=diag, compare_op=ALU.is_ge, fill=MASKED, base=0,
                                        pattern=[[0, 2 if k % 3 else NJ], [-1, P]],
                                        channel_multiplier=1).then_inc(sc_masked, 1)

            def mask(group, p):
                pool.wait_ge(exp_done, PAIRS * group + p + 1)
                pool.sem_inc(waited)
                diag = pt[:, p % SLOTS, :, 0:2 * P]
                nc.gpsimd.affine_select(out=diag, in_=diag, compare_op=ALU.is_ge, fill=0.0, base=0,
                                        pattern=[[0, 2], [0, 2], [1, P]], channel_multiplier=-1).then_inc(p_masked, 1)

            def step(n, group, par):
                count = x_count(n, 1 - par)
                if group is None:
                    inverse_deviation(n)
                    nc.gpsimd.memset(kbd[0:ONE].bitcast(F32), 0.0).then_inc(c_kzero, 1)
                    pool.wait_ge(d_bias, 16 * 4)
                    xres_of(n, 1 - par, count)
                    nc.gpsimd.memset(mcol[:], 0.0).then_inc(c_mcol, 1)
                    value_padding(pool, 1)
                    for k in range(2, CHUNKS):
                        split_experts(pool, k, 0)
                        split_experts(pool, k, 1)
                    inverse_deviation(n + 1)
                    for k in range(NG * UNITS):
                        mask_scores(n, k)
                    return
                for p in range(PAIRS):
                    mask(group, p)
                if n is not None:
                    xres_of(n, 1 - par, count)
                    if has_next(n):
                        inverse_deviation(n + 1)
                    for k in range(NG * UNITS):
                        mask_scores(n, k)

            over_groups(pool, step)

        @block.scalar
        def _(act):
            def exp_pair(group, p):
                act.wait_ge(kq_scores, PAIRS * group + p + 1)
                nc.scalar.activation(pt[:, p % SLOTS], A[p % 2][:, :, 0:3 * P], ACT.Exp, scale=SCALE)\
                  .then_inc(exp_done, 1)

            def rows_of_max(n, par, c):
                act.wait_ge(mT_full, NC * n + c + 1)
                for i in range(2):
                    nc.scalar.activation(qst[par][ONE:ONE + ROWS_M, 2 * c + i, :],
                                         bank(("mT", c))[P // 2 * i:P // 2 * i + ROWS_M, :], ACT.Copy).then_inc(m_rows, 1)

            def exp_gap(n):
                act.wait_ge(routed, ROUTE * n + 2 * NT + 2)
                nc.scalar.activation(expgap[:], gap[:], ACT.Exp).then_inc(gap_exp, 1)

            def copy_columns(group):
                act.wait_ge(onT_full, group + 1)
                nc.scalar.activation(onT[:], bank(("onT", 0))[:], ACT.Copy).then_inc(onT_copied, 1)

            def copy_rows(n, par, slot):
                g, r = divmod(slot, SLOTS_G)
                if g > 0 and g % 2 == 0 and r == ROWS_AT:
                    rows_of_max(n, par, g // 2 - 1)

            def copy_scores(n, slot):
                if slot < NG * SLOTS_G:
                    for k in range(PER_SLOT * slot, PER_SLOT * (slot + 1)):
                        act.wait_ge(qk_scores, NG * UNITS * n + k + 1)
                        if k >= RING:
                            act.wait_ge(max_done, NG * UNITS * n + k + 1 - RING)
                        nc.scalar.activation(sc[:, k % RING], bank(("scores", k))[:], ACT.Copy).then_inc(sc_copied, 1)

            def step(n, group, par):
                if group is None:
                    act.wait_ge(c_onecol, 1)

                    def ones_of_k(j):
                        nc.scalar.activation(kbd[ONE:ONE + ROWS_M, j].rearrange("p g t -> p (g t)"),
                                             onecol[ONE:ONE + ROWS_M, j:j + 1].broadcast_to([ROWS_M, NG * T]),
                                             ACT.Copy).then_inc(c_kzero, 1)

                    ones_of_k(0)
                    ones_of_k(1)
                    act.wait_ge(wT_copied, 2 * NC)
                    nc.scalar.activation(wqkhi[:], wqk[:], ACT.Copy).then_inc(wqk_hi, 1)
                    ones_of_k(2)
                    ones_of_k(3)
                    for k in range(CHUNKS):
                        at = chunk(k)
                        for hi, raw, there in ((w1hi, w1raw, d_w1[k]), (w3hi, w3raw, d_w3[k])):
                            act.wait_ge(there, 32 if k == CHUNKS - 1 else 16)
                            nc.scalar.activation(hi[:, at], raw[:, at], ACT.Copy).then_inc(wexp_hi, 1)
                        if k == 0:
                            exp_gap(n)
                else:
                    for p in range(EARLY, PAIRS):
                        exp_pair(group, p)
                        if p == GAP_AT and n is not None:
                            exp_gap(n)
                if n is None:
                    copy_columns(group)
                    return
                for s in range(STEPS):
                    if s >= FIRST:
                        copy_rows(n, 1 - par, s - FIRST)
                    act.wait_ge(h1_full, STEPS * n + s + 1)
                    nc.scalar.activation(act1[s % 2][:], A[s % 2][:, 0, :], ACT.Silu).then_inc(silu_done, 1)
                    if s == 3 and group is not None:
                        copy_columns(group)
                    if s >= FIRST:
                        copy_scores(n, s - FIRST)
                for p in range(EARLY):
                    exp_pair(n, p)
                copy_rows(n, 1 - par, MAX_SLOTS - 1)

            over_groups(act, step)

        @block.vector
        def _(dve):

            def attention_weights():
                dve.wait_ge(wT_ready, 1)
                for src, dst in ((A[0][:, 0, 0:P], wqk[:, 0, :]), (A[0][:, 0, P:2 * P], wqk[:, 1, :]),
                                 (ident[:], order[:])):
                    for c in range(NC):
                        nc.vector.tensor_copy(
                            dst.rearrange("p (j d c i) -> p c j i d", j=NJ, d=HD, c=NC)[:, c],
                            src[:, c * P // NC:(c + 1) * P // NC].rearrange("p (j i d) -> p j i d", j=NJ, d=HD))\
                          .then_inc(wT_copied, 1)
                nc.vector.tensor_copy(wvr[:, 0:P], A[0][:, 0, 2 * P:3 * P]).then_inc(wT_copied, 1)
                nc.vector.tensor_copy(woT[:], A[0][:, 0, 3 * P:4 * P]).then_inc(wT_copied, 1)

            def attention_weights_lo():
                dve.wait_ge(wqk_hi, 1)
                nc.vector.tensor_tensor(wqklo[:], wqk[:], wqkhi[:].bitcast(F32), ALU.subtract).then_inc(wqk_split, 1)

            def copy_o(group, c):
                dve.wait_ge(o_full, NC * group + c + 1)
                nc.vector.tensor_copy(oT[:, c, :], Y[c][:]).then_inc(o_copied, 1)

            def one_columns():
                dve.wait_ge(c_ident, 2)
                nc.vector.tensor_reduce(onecol[:], ident[:, ONE:ONE + ROWS_M].rearrange("p (j r) -> p j r", r=2),
                                        AX.X, ALU.add).then_inc(c_onecol, 1)

            def norm_stats(n, par, count):
                dve.wait_ge(x_in[par], count)
                for t in range(NT):
                    nc.vector.bn_stats(stats[:, t, :], xin[par][:, t, :]).then_inc(stats_done, 1)
                dve.wait_ge(stats_done, NT * (n + 1))
                dve.sem_inc(waited)
                for t in range(NT):
                    nc.vector.bn_aggr(mv[:, t, :], stats[:, t, :]).then_inc(mv_done, 1)
                dve.wait_ge(mv_done, NT * (n + 1))
                nc.vector.tensor_scalar(vareps[:], mv[:, :, 1], EPS, None, ALU.add).then_inc(var_done, 1)

            def norm_apply(n, par):
                dve.wait_ge(rstd_done, n + 1)
                for t in range(NT):
                    nc.vector.tensor_scalar(xn[:, t, :], xin[par][:, t, :], mv[:, t, 0:1], rstd[:, t:t + 1],
                                            ALU.subtract, ALU.mult).then_inc(xn_done, 1)

            def copy_x(n, par):
                dve.wait_ge(xT_full, n + 1)
                nc.vector.tensor_copy(xT[par][:], bank(("xT", 0))[:]).then_inc(xT_copied, 1)

            def split_x(n, par):
                dve.wait_ge(xT_copied, n + 1)
                nc.vector.tensor_copy(xThi[par][:], xT[par][:]).then_inc(xT_hi, 1)
                dve.wait_ge(xT_hi, n + 1)
                nc.vector.tensor_tensor(xTlo[par][:], xT[par][:], xThi[par][:].bitcast(F32),
                                        ALU.subtract).then_inc(xT_split, 1)

            def split_qk(n, o):
                dve.wait_ge(qk_full, 2 * n + o + 1)
                if o == 0 and not (isinstance(n, int) and n == 0):
                    dve.wait_ge(qk_stacked, STACKS * n)
                nc.vector.tensor_scalar(qkhi[o][:], bank(("qk", o))[:], bqk[:, o:o + 1], None,
                                        ALU.add).then_inc(qk_hi, 1)
                dve.wait_ge(qk_hi, 2 * n + o + 1)
                nc.vector.scalar_tensor_tensor(out=qklo[o][:], in0=bank(("qk", o))[:], scalar=bqk[:, o:o + 1],
                                               in1=qkhi[o][:].bitcast(F32), op0=ALU.add, op1=ALU.subtract)\
                  .then_inc(qk_split, 1)

            def copy_v(n, par, k):
                dve.wait_ge(vr_full, 2 * n + k + 1)
                src = bank(("vr", k))[:, 0:2 * (P + E)].rearrange("p (t c) -> p t c", t=2)
                for t in range(2):
                    last = nc.vector.tensor_tensor(va[par][:, 2 * k + t, :, 0:3:2, 0:HD],
                                                   src[:, t, 0:P].rearrange("p (h i d) -> p h i d", i=2, d=HD),
                                                   bv_b[:].rearrange("p (h i d) -> p h i d", i=2, d=HD), ALU.add)
                last.then_inc(v_copied, 1)
                nc.vector.tensor_copy(lg[par][:, 2 * k:2 * k + 2, :], src[:, :, P:P + E]).then_inc(lg_copied, 1)

            def route_top(n, par):
                dve.wait_ge(lg_copied, 2 * (n + 1))
                dve.sem_inc(waited)
                for t in range(NT):
                    nc.vector.max(top[:, t, :], lg[par][:, t, :]).then_inc(routed, 1)
                dve.wait_ge(routed, ROUTE * n + NT)
                dve.sem_inc(waited)
                for t in range(NT):
                    nc.vector.max_index(topi[:, t, :], top[:, t, :], lg[par][:, t, :]).then_inc(routed, 1)
                dve.wait_ge(routed, ROUTE * n + 2 * NT)
                nc.vector.tensor_copy(topf[:], topi[:]).then_inc(routed, 1)
                nc.vector.tensor_tensor(gap[:], top[:, :, 1], top[:, :, 0], ALU.subtract).then_inc(routed, 1)

            def route_gates(n):
                k = ROUTE * n + 2 * NT + 2
                dve.wait_ge(routed, k)
                for hot, which in ((hot1, 0), (hot2, 1)):
                    nc.vector.tensor_tensor(hot[:], iota8[:].unsqueeze(1).broadcast_to([P, NT, E]),
                                            topf[:, :, which:which + 1].broadcast_to([P, NT, E]),
                                            ALU.is_equal).then_inc(routed, 1)
                dve.wait_ge(gap_exp, n + 1)
                nc.vector.tensor_scalar(gden[:], expgap[:], 1.0, None, ALU.add).then_inc(routed, 1)
                dve.wait_ge(routed, k + 3)
                nc.vector.reciprocal(gate1[:], gden[:]).then_inc(routed, 1)
                dve.wait_ge(routed, k + 4)
                nc.vector.tensor_tensor(cw1[:], hot1[:], gate1[:].unsqueeze(2).broadcast_to([P, NT, E]),
                                        ALU.mult)
                nc.vector.tensor_tensor(gate2[:], expgap[:], gate1[:], ALU.mult).then_inc(routed, 1)
                dve.wait_ge(routed, k + 5)
                nc.vector.tensor_tensor(cw2[:], hot2[:], gate2[:].unsqueeze(2).broadcast_to([P, NT, E]),
                                        ALU.mult).then_inc(routed, 1)
                dve.wait_ge(routed, k + 6)
                nc.vector.tensor_tensor(cw[:], cw1[:], cw2[:], ALU.add).then_inc(routed, 1)

            def row_maxima(n, k):
                b, u = divmod(k % UNITS, 3)
                g = k // UNITS
                src = sc[:, k % RING]
                dve.wait_ge(sc_masked, UNITS * NG * n + k + 1)
                if u == 0:
                    o, i = mx[:, g, QT * b, :], src.rearrange("p (j k) -> p j k", j=NJ)
                else:
                    o, i = mx[:, g, QT * b + 1, 2 * u - 2:2 * u], src.rearrange("p (j k) -> p j k", j=2)
                nc.vector.reduce_max(o, i, AX.X).then_inc(max_done, 1)

            def split_max(n, g):
                cols = mcol[:, g // 2, :, g % 2, 0:ROWS_M].rearrange("p t (j r) -> p t j r", r=2)
                hi, lo = cols[:, :, :, 0], cols[:, :, :, 1]
                dve.wait_ge(max_done, UNITS * (NG * n + g + 1))
                nc.vector.tensor_scalar(hi.bitcast(F32R), mx[:, g], -1.0, None, ALU.mult).then_inc(m_split, 1)
                dve.wait_ge(m_split, 2 * (NG * n + g) + 1)
                nc.vector.scalar_tensor_tensor(out=lo.bitcast(F32R), in0=mx[:, g], scalar=-1.0, in1=hi, op0=ALU.mult,
                                               op1=ALU.subtract).then_inc(m_split, 1)

            def maxima(n, slot):
                g, k = divmod(slot, SLOTS_G)
                if g < NG:
                    for u in range(PER_SLOT):
                        row_maxima(n, PER_SLOT * slot + u)
                    if k == SLOTS_G - 1:
                        split_max(n, g)

            def normalise(group, k):
                src = bank(("oN", k))[:].rearrange("p (t r) -> p t r", r=HALF)
                r = rec[:, 2 * k:2 * k + 2, :].rearrange("p t h -> p (t h)")
                dve.wait_ge(oN_full, NT // 2 * group + k + 1)
                nc.vector.reciprocal(r, src[:, :, HD]).then_inc(rec_done, 1)
                dve.wait_ge(rec_done, NT // 2 * group + k + 1)
                nc.vector.tensor_tensor(on[:, 2 * k:2 * k + 2, :].rearrange("p t (h d) -> p (t h) d", d=HD),
                                        src[:, :, 0:HD], r.unsqueeze(2).broadcast_to([P, 2 * H, HD]),
                                        ALU.mult).then_inc(on_done, 1)

            def hidden(n, s):
                dve.wait_ge(h3_full, STEPS * n + s + 1)
                dve.wait_ge(silu_done, STEPS * n + s + 1)
                nc.vector.tensor_tensor(hid[s // NH % 2][:, s % NH, :], act1[s % 2][:], A[s % 2][:, 1, :],
                                        ALU.mult).then_inc(hid_done, 1)

            def add_expert(n, par, e):
                dve.wait_ge(y_full, NE * n + e + 1)
                if e == 0:
                    dve.wait_ge(xres_done, n + 1)
                    dve.wait_ge(stored[par], 16 + 8 * n - (8 if par else 0))
                if e < E:
                    for t in range(NT):
                        if e > 0:
                            dve.wait_ge(y_added, YADDS * n + NT * (e - 1) + t + 1)
                        before = xres[par] if e == 0 else res[par]
                        nc.vector.scalar_tensor_tensor(out=res[par][:, t, :], in0=Y[e % 2][:, t * D:(t + 1) * D],
                                                       scalar=cw[:, t, e:e + 1], in1=before[:, t, :],
                                                       op0=ALU.mult, op1=ALU.add).then_inc(y_added, 1)
                else:
                    dve.wait_ge(y_added, YADDS * n + NT * E)
                    nc.vector.tensor_tensor(res[par][:], res[par][:], Y[e % 2][:].rearrange("p (t d) -> p t d", d=D),
                                            ALU.add).then_inc(y_added, 1)

            def add_attention(group, par):
                dve.wait_ge(attn_full, group + 1)
                dve.wait_ge(y_added, YADDS * (group + 1))
                nc.vector.tensor_tensor(res[par][:], res[par][:], Y[1][:].rearrange("p (t d) -> p t d", d=D),
                                        ALU.add).then_inc(attn_added, 1)

            def step(n, group, par):
                if group is None:
                    one_columns()
                    value_padding(dve, 0)
                    norm_stats(n, 1 - par, x_count(n, 1 - par))
                    norm_apply(n, 1 - par)
                    attention_weights()
                if n is not None:
                    copy_x(n, 1 - par)
                    if group is None:
                        attention_weights_lo()
                    split_x(n, 1 - par)
                    if group is None:
                        dve.wait_ge(d_bias, 16 * 4)
                    copy_v(n, 1 - par, 0)
                    copy_v(n, 1 - par, 1)
                    route_top(n, 1 - par)
                    if group is None:
                        split_experts(dve, 0, 0)
                        dve.wait_ge(bias_full, 1)
                        nc.vector.tensor_copy(bqk[:], A[1][:, 0, 0:2]).then_inc(bias_ready, 1)
                        dve.wait_ge(bias_ready, 1)
                    split_qk(n, 0)
                    if group is None:
                        split_experts(dve, 0, 1)
                    split_qk(n, 1)
                if group is not None:
                    copy_o(group, 0)
                if n is None:
                    copy_o(group, 1)
                    normalise(group, 0)
                    normalise(group, 1)
                    add_attention(group, par)
                    return
                route_gates(n)
                for e in range(NE):
                    for hh in range(NH):
                        s = NH * e + hh
                        hidden(n, s)
                        if group is None:
                            if s == 0:
                                split_experts(dve, 1, 0)
                                split_experts(dve, 1, 1)
                            if s == FIRST:
                                dve.wait_ge(c_mcol, 1)
                                dve.wait_ge(c_va[1], 2)
                        else:
                            if s == 0:
                                copy_o(group, NC - 1)
                            if s in (1, 2):
                                normalise(group, s - 1)
                        if has_next(n):
                            if s == 3:
                                norm_stats(n + 1, par, x_count(n + 1, par))
                            if s == 4:
                                norm_apply(n + 1, par)
                        if s == 4 and group is not None:
                            add_attention(group, par)
                        if s > FIRST:
                            maxima(n, s - FIRST - 1)
                    if e > 0:
                        add_expert(n, 1 - par, e - 1)
                add_expert(n, 1 - par, NE - 1)

            over_groups(dve, step)

        @block.tensor
        def _(pe):
            pe.wait_ge(c_ident, 2)
            pe.wait_ge(d_watt, 16 * 5)
            for k in range(4):
                last = nc.tensor.transpose(A[0][:, 0, k * P:(k + 1) * P], wraw[:, k, :], ident[:])
            last.then_inc(wT_ready, 1)

            def three(o, hi, lo, xhi, xlo):
                nc.tensor.matmul(o, hi, xhi, start=True, stop=False)
                nc.tensor.matmul(o, hi, xlo, start=False, stop=False)
                return nc.tensor.matmul(o, lo, xhi, start=False, stop=True)

            def transpose_x(n, group):
                bank_free(pe, ("xT", 0), n, group)
                pe.wait_ge(xn_done, NT * (n + 1))
                for t in range(NT):
                    last = nc.tensor.transpose(bank(("xT", 0))[:, t * P:(t + 1) * P], xn[:, t, :], ident[:])
                last.then_inc(xT_full, 1)

            def project_qk(n, group, par):
                pe.wait_ge(xT_split, n + 1)
                for o in range(2):
                    bank_free(pe, ("qk", o), n, group)
                    three(bank(("qk", o))[:], wqkhi[:, o, :], wqklo[:, o, :], xThi[par][:], xTlo[par][:])\
                        .then_inc(qk_full, 1)

            def project_v(n, group, par):
                pe.wait_ge(xT_copied, n + 1)
                for k in range(2):
                    bank_free(pe, ("vr", k), n, group)
                    for t in range(2):
                        last = nc.tensor.matmul(bank(("vr", k))[:, t * (P + E):(t + 1) * (P + E)],
                                                xT[par][:, (2 * k + t) * P:(2 * k + t + 1) * P], wvr[:],
                                                start=True, stop=True)
                    last.then_inc(vr_full, 1)

            def scores(n, group, par, k):
                g = k // UNITS
                b, u = divmod(k % UNITS, 3)
                if k == 0:
                    pe.wait_ge(qk_stacked, STACKS * (n + 1))
                o = bank(("scores", k))
                bank_free(pe, ("scores", k), n, group)
                at = b * S + (P if u else 0)
                q, keys = qst[par][0:ONE, g, at:at + P], kbd[0:ONE, :, g]
                if u == 0:
                    last = nc.tensor.matmul(o[:].rearrange("p (j k) -> p j k", j=NJ), q, keys[:, :, at:at + P],
                                            start=True, stop=True)
                else:
                    last = nc.tensor.matmul(o[:].rearrange("p (j k) -> p j k", j=2), q,
                                            keys[:, 2 * u - 2:2 * u, b * S:(b + 1) * S], start=True, stop=True)
                last.then_inc(qk_scores, 1)

            def transpose_max(n, group, c):
                bank_free(pe, ("mT", c), n, group)
                pe.wait_ge(m_split, 2 * (NG * n + 2 * c + 2))
                for t in range(NT):
                    last = nc.tensor.transpose(bank(("mT", c))[:, t * P:(t + 1) * P],
                                               mcol[:, c, t].rearrange("p i r -> p (i r)"), ident[:])
                last.then_inc(mT_full, 1)

            def prepare_maxima(n, group, par, slot):
                if slot < NG * SLOTS_G:
                    for k in range(PER_SLOT * slot, PER_SLOT * (slot + 1)):
                        scores(n, group, par, k)

            def prepare_rows(n, group, slot):
                g, k = divmod(slot, SLOTS_G)
                if g > 0 and g % 2 == 0 and k == ROWS_AT:
                    transpose_max(n, group, g // 2 - 1)

            def of_pair(p):
                g, r = divmod(p, SEQS * 2)
                return g, r // 2, (r % 2) * 2

            def pair_scores(group, par, p):
                g, b, j0 = of_pair(p)
                if p < 2:
                    pe.wait_ge(hid_done, STEPS * (group + 1) + p - 1)
                if p % 4 == 0:
                    pe.wait_ge(m_rows, NG * group + g + 1)
                if p >= 2:
                    pe.wait_ge(exp_done, PAIRS * group + p - 1)
                keys = kbd[0:ONE + ROWS_M, :, g]
                for a in range(2):
                    o = A[p % 2][:, a, 0:3 * P].rearrange("p (c q) -> p c q", q=P)
                    for kt, columns in ((1, o[:, 0:2]), (0, o[:, 0:3:2])):
                        last = nc.tensor.matmul(columns, keys[:, j0 + a, b * S + kt * P:b * S + (kt + 1) * P],
                                                qst[par][0:ONE + ROWS_M, g, b * S:(b + 1) * S].rearrange("p (c q) -> p c q", q=P),
                                                start=True, stop=True)
                last.then_inc(kq_scores, 1)

            def pair_outputs(group, par, p):
                g, b, _ = of_pair(p)
                c, i = divmod(g, 2)
                if p == 0:
                    pe.wait_ge(v_copied, 2 * (group + 1))
                    pe.wait_ge(y_added, YADDS * (group + 1))
                for kt in range(QT):
                    for j in range(NJ):
                        pair = p + j // 2
                        if kt == 0 and j % 2 == 0:
                            pe.wait_ge(p_masked, PAIRS * group + pair + 1)
                        o = Y[c][ROWS * j:ROWS * (j + 1), b * S:(b + 1) * S]
                        v = va[par][:, QT * b + kt, NJ * c + j, i:i + 2].rearrange("p a r -> p (a r)")
                        pr = pt[:, pair % SLOTS, j % 2, :].rearrange("p (c q) -> p c q", q=P)
                        if kt == 0:
                            nc.tensor.matmul(o.rearrange("p (c q) -> p c q", q=P), v, pr[:, 0:3:2],
                                             start=(i == 0 and b == 0), stop=False)
                        else:
                            last = nc.tensor.matmul(o[:, P:2 * P], v, pr[:, 1], start=False,
                                                    stop=(i == 1 and b == SEQS - 1))
                if p % (PAIRS // NC) == PAIRS // NC - 2:
                    last.then_inc(o_full, 1)

            def up(n, group, par, s):
                e, hh = divmod(s, NH)
                if s >= 2:
                    pe.wait_ge(hid_done, STEPS * n + s - 1)
                elif group is not None:
                    pe.wait_ge(exp_done, PAIRS * (group + 1) - 1 + s)
                new_part = group is None and hh == 0 and e * CHUNKS % NE == 0
                if new_part:
                    pe.wait_ge(wexp_split[e * CHUNKS // NE], 1)
                c = slice(hh * P, (hh + 1) * P)
                three(A[s % 2][:, 0, :], w1hi[:, e, c], w1lo[:, e, c], xThi[par][:], xTlo[par][:])\
                    .then_inc(h1_full, 1)
                if new_part:
                    pe.wait_ge(wexp_split[e * CHUNKS // NE], 2)
                three(A[s % 2][:, 1, :], w3hi[:, e, c], w3lo[:, e, c], xThi[par][:], xTlo[par][:])\
                    .then_inc(h3_full, 1)

            def down(n, group, e):
                if e >= 2:
                    pe.wait_ge(y_added, YADDS * n + NT * (e - 1))
                elif group is not None:
                    if e == 0:
                        pe.wait_ge(o_copied, NC * (group + 1) - 1)
                    else:
                        pe.wait_ge(attn_added, group + 1)
                elif e == 0:
                    pe.wait_ge(d_w2, 16 * NE)
                pe.wait_ge(hid_done, STEPS * n + NH * (e + 1))
                for t in range(NT):
                    for hh in range(NH):
                        last = nc.tensor.matmul(Y[e % 2][:, t * D:(t + 1) * D], hid[e % 2][:, hh, t * P:(t + 1) * P],
                                                w2s[:, e, hh, :], start=(hh == 0), stop=(hh == NH - 1))
                last.then_inc(y_full, 1)

            def output_projection(group):
                pe.wait_ge(onT_copied, group + 1)
                pe.wait_ge(o_copied, NC * (group + 1))
                for t in range(NT):
                    last = nc.tensor.matmul(Y[1][:, t * D:(t + 1) * D], onT[:, t * P:(t + 1) * P], woT[:],
                                            start=True, stop=True)
                last.then_inc(attn_full, 1)

            def attention_rows(n, group, k):
                bank_free(pe, ("oN", k), n, group)
                if k == 0:
                    pe.wait_ge(o_copied, NC * (group + 1))
                for t in range(2):
                    for c in range(NC):
                        last = nc.tensor.transpose(bank(("oN", k))[:, (NC * t + c) * P:(NC * t + c + 1) * P],
                                                   oT[:, c, (2 * k + t) * P:(2 * k + t + 1) * P], ident[:])
                last.then_inc(oN_full, 1)

            def attention_columns(n, group):
                bank_free(pe, ("onT", 0), n, group)
                pe.wait_ge(on_done, NT // 2 * (group + 1))
                for t in range(NT):
                    last = nc.tensor.transpose(bank(("onT", 0))[:, t * P:(t + 1) * P], on[:, t, :], ident[:])
                last.then_inc(onT_full, 1)

            def step(n, group, par):
                if group is None:
                    transpose_x(n, group)
                    pe.wait_ge(wT_copied, 3 * NC + 2)
                    project_v(n, group, 1 - par)
                    pe.wait_ge(d_bias, 16 * 4)
                    nc.tensor.matmul(A[1][:, 0, 0:2], order[:], braw[:], start=True, stop=True).then_inc(bias_full, 1)
                    pe.wait_ge(wqk_split, 1)
                    project_qk(n, group, 1 - par)
                else:
                    lag = 4
                    for p in range(EARLY, PAIRS + lag, 2):
                        if p == PAIRS + lag - 2 and n is not None:
                            up(n, group, 1 - par, 0)
                        if p >= lag:
                            pair_outputs(group, par, p - lag)
                        if p == X_AT and n is not None:
                            transpose_x(n, group)
                        if p < PAIRS:
                            pair_scores(group, par, p)
                            pair_scores(group, par, p + 1)
                        if n is not None:
                            if p == V_AT:
                                project_v(n, group, 1 - par)
                            if p == QK_AT:
                                project_qk(n, group, 1 - par)
                if n is None:
                    attention_rows(n, group, 0)
                    attention_rows(n, group, 1)
                    attention_columns(n, group)
                    output_projection(group)
                    return
                for e in range(NE):
                    for hh in range(NH):
                        s = NH * e + hh
                        if s >= FIRST:
                            prepare_rows(n, group, s - FIRST)
                        if s > 0 or group is None:
                            up(n, group, 1 - par, s)
                        if group is not None:
                            if s in (1, 2):
                                attention_rows(n, group, s - 1)
                            if s == 3:
                                attention_columns(n, group)
                            if s == 4:
                                output_projection(group)
                        if s >= FIRST:
                            prepare_maxima(n, group, 1 - par, s - FIRST)
                    if e > 0:
                        down(n, group, e - 1)
                prepare_rows(n, group, MAX_SLOTS - 1)
                if group is None:
                    pe.wait_ge(c_va[0], 2)
                    pe.wait_ge(c_va[1], 2)
                for p in range(EARLY):
                    pair_scores(n, 1 - par, p)
                down(n, group, NE - 1)

            over_groups(pe, step)


_INS = ["L0_attn_x", "L0_attn_Wq", "L0_attn_bq", "L0_attn_Wk", "L0_attn_bk", "L0_attn_Wv", "L0_attn_bv", "L0_attn_Wo",
        "L0_attn_bo", "L0_ffn_w_router", "L0_ffn_w1", "L0_ffn_w3", "L0_ffn_w2", "L0_ffn_sw1", "L0_ffn_sw3",
        "L0_ffn_sw2"]


def kernel(**inputs):
    import numpy as _np
    import concourse.bacc as _bacc
    from concourse.bass_utils import run_bass_kernel_spmd as _run

    nc = _bacc.Bacc("TRN2", target_bir_lowering=False, num_devices=1)
    arrays, args = {}, []
    for name in _INS:
        a = _np.ascontiguousarray(inputs[name])
        arrays[f"in_{name}"] = a
        args.append(nc.dram_tensor(f"in_{name}", a.shape, mybir.dt.from_np(a.dtype), kind="ExternalInput").ap())
    shape = arrays["in_L0_attn_x"].shape
    args.append(nc.dram_tensor("out_0", shape, F32, kind="ExternalOutput").ap())
    program(nc, *args)
    r = _run(nc, [arrays], core_ids=[0])
    return r.results[0]["out_0"]
```
